# Optimizing a Trainium2 kernel written in Bass

```python
import numpy as np
import jax
import jax.numpy as jnp

def _softmax(x, axis=-1):
    return jax.nn.softmax(x, axis=axis)

def _gelu(x):
    return jax.nn.gelu(x, approximate=True)

def _silu(x):
    return jax.nn.silu(x)

def _sigmoid(x):
    return jax.nn.sigmoid(x)

def _layernorm(x, axis=-1, eps=1e-05):
    m = jnp.mean(x, axis=axis, keepdims=True)
    v = jnp.var(x, axis=axis, keepdims=True)
    return (x - m) / jnp.sqrt(v + eps)

def _scatter_add(tgt, idx, src, axis=0):
    return tgt.at[idx].add(src)

def _segment_sum(src, seg, n):
    return jax.ops.segment_sum(src, seg, n)
kernel_name = 'mk_prb_d2_jaxref_r8_b37d3e'

def setup_inputs(seed: int=0):
    np.random.seed(seed)
    _w = jnp.asarray

    def _L0_attn_setup():
        import jax, jax.numpy as jnp
        import numpy as np
        HEADS = 16
        KV_GROUPS = 4
        SWA_SIZE = 128
        NEG_INF = jnp.float32(-1e+30)
        key = jax.random.key(seed)
        ks = jax.random.split(key, 6)
        B, T, E, M = (1, 512, 256, 256)
        Dkv = M // HEADS * KV_GROUPS
        s = lambda fan: 1.0 / np.sqrt(fan)
        return {'x': jax.random.normal(ks[0], (B, T, E), jnp.float32), 'Wq': jax.random.normal(ks[1], (E, M), jnp.float32) * s(E), 'Wk': jax.random.normal(ks[2], (E, Dkv), jnp.float32) * s(E), 'Wv': jax.random.normal(ks[3], (E, Dkv), jnp.float32) * s(E), 'Wo': jax.random.normal(ks[4], (M, M), jnp.float32) * s(M), 'bo': jnp.zeros((M,), jnp.float32)}
    _L0_attn_in = _L0_attn_setup()

    def _L0_ffn_setup():
        import jax, jax.numpy as jnp
        import numpy as np
        B, L, D = (2, 128, 256)
        E, TOP_K, RANK, DFF = (8, 2, 8, 688)

        def _lora(x, A, Bm, scale):
            return x @ A @ Bm * scale

        def _expert_lora(x, A, Bm, w, scale):
            xA = jnp.einsum('bld,edr->bler', x, A)
            xAB = jnp.einsum('bler,erd->bled', xA, Bm) * scale
            return (xAB * w).sum(axis=2)
        key = jax.random.key(seed)
        ks = jax.random.split(key, 18)
        r = lambda k, s, sc: jax.random.normal(k, s, dtype=jnp.float32) * sc
        inv_d = 1.0 / np.sqrt(D)
        inv_f = 1.0 / np.sqrt(DFF)
        return {'x': r(ks[0], (B, L, D), 1.0), 'W_router': r(ks[1], (D, E), inv_d), 'W_gate': r(ks[2], (D, DFF), inv_d), 'W_up': r(ks[3], (D, DFF), inv_d), 'W_down': r(ks[4], (DFF, D), inv_f), 'sA_gate': r(ks[5], (D, RANK), inv_d), 'sB_gate': r(ks[6], (RANK, DFF), 0.02), 'sA_up': r(ks[7], (D, RANK), inv_d), 'sB_up': r(ks[8], (RANK, DFF), 0.02), 'sA_down': r(ks[9], (DFF, RANK), inv_f), 'sB_down': r(ks[10], (RANK, D), 0.02), 'A_gate': r(ks[11], (E, D, RANK), inv_d), 'B_gate': r(ks[12], (E, RANK, DFF), 0.02), 'A_up': r(ks[13], (E, D, RANK), inv_d), 'B_up': r(ks[14], (E, RANK, DFF), 0.02), 'A_down': r(ks[15], (E, DFF, RANK), inv_f), 'B_down': r(ks[16], (E, RANK, D), 0.02), 'expert_bias': jnp.zeros((E,), dtype=jnp.float32)}
    _L0_ffn_in = _L0_ffn_setup()

    def _L1_attn_setup():
        import jax, jax.numpy as jnp
        import numpy as np
        HIDDEN = 256
        KEY = 256
        EPS = 1e-05
        key = jax.random.key(seed)
        k1, k2, k3 = jax.random.split(key, 3)
        B, S = (4, 256)
        x = jax.random.normal(k1, (B, S, HIDDEN), dtype=jnp.float32)
        bq = 1.0 / np.sqrt(HIDDEN)
        qkv = jax.random.uniform(k2, (HIDDEN, KEY * 3), minval=-bq, maxval=bq, dtype=jnp.float32)
        bo = 1.0 / np.sqrt(KEY)
        o_proj = jax.random.uniform(k3, (KEY, HIDDEN), minval=-bo, maxval=bo, dtype=jnp.float32)
        gamma = jnp.ones((HIDDEN,), dtype=jnp.float32)
        beta = jnp.zeros((HIDDEN,), dtype=jnp.float32)
        return {'x': x, 'qkv': qkv, 'o_proj': o_proj, 'gamma': gamma, 'beta': beta}
    _L1_attn_in = _L1_attn_setup()

    def _L1_ffn_setup():
        import jax, jax.numpy as jnp
        import numpy as np
        B, S, H = (1, 64, 256)
        I = 192
        E = 32
        K = 4
        SCALE = 1.8
        key = jax.random.key(seed)
        ks = jax.random.split(key, 9)
        init = lambda k, shape: jax.random.normal(k, shape, jnp.float32) * (1.0 / np.sqrt(shape[-1]))
        return {'x': jax.random.normal(ks[0], (B, S, H), jnp.float32), 'router_w': init(ks[1], (E, H)), 'router_b': jnp.zeros((E,), jnp.float32), 'gate_w': init(ks[2], (E, I, H)), 'up_w': init(ks[3], (E, I, H)), 'down_w': init(ks[4], (E, H, I)), 'shared_gate_w': init(ks[5], (I, H)), 'shared_up_w': init(ks[6], (I, H)), 'shared_down_w': init(ks[7], (H, I))}
    _L1_ffn_in = _L1_ffn_setup()
    _d = {'L0_attn_x': _L0_attn_in['x'], 'L0_attn_Wq': _L0_attn_in['Wq'], 'L0_attn_Wk': _L0_attn_in['Wk'], 'L0_attn_Wv': _L0_attn_in['Wv'], 'L0_attn_Wo': _L0_attn_in['Wo'], 'L0_attn_bo': _L0_attn_in['bo'], 'L0_ffn_W_router': _L0_ffn_in['W_router'], 'L0_ffn_W_gate': _L0_ffn_in['W_gate'], 'L0_ffn_W_up': _L0_ffn_in['W_up'], 'L0_ffn_W_down': _L0_ffn_in['W_down'], 'L0_ffn_sA_gate': _L0_ffn_in['sA_gate'], 'L0_ffn_sB_gate': _L0_ffn_in['sB_gate'], 'L0_ffn_sA_up': _L0_ffn_in['sA_up'], 'L0_ffn_sB_up': _L0_ffn_in['sB_up'], 'L0_ffn_sA_down': _L0_ffn_in['sA_down'], 'L0_ffn_sB_down': _L0_ffn_in['sB_down'], 'L0_ffn_A_gate': _L0_ffn_in['A_gate'], 'L0_ffn_B_gate': _L0_ffn_in['B_gate'], 'L0_ffn_A_up': _L0_ffn_in['A_up'], 'L0_ffn_B_up': _L0_ffn_in['B_up'], 'L0_ffn_A_down': _L0_ffn_in['A_down'], 'L0_ffn_B_down': _L0_ffn_in['B_down'], 'L0_ffn_expert_bias': _L0_ffn_in['expert_bias'], 'L1_attn_qkv': _L1_attn_in['qkv'], 'L1_attn_o_proj': _L1_attn_in['o_proj'], 'L1_attn_gamma': _L1_attn_in['gamma'], 'L1_attn_beta': _L1_attn_in['beta'], 'L1_ffn_router_w': _L1_ffn_in['router_w'], 'L1_ffn_router_b': _L1_ffn_in['router_b'], 'L1_ffn_gate_w': _L1_ffn_in['gate_w'], 'L1_ffn_up_w': _L1_ffn_in['up_w'], 'L1_ffn_down_w': _L1_ffn_in['down_w'], 'L1_ffn_shared_gate_w': _L1_ffn_in['shared_gate_w'], 'L1_ffn_shared_up_w': _L1_ffn_in['shared_up_w'], 'L1_ffn_shared_down_w': _L1_ffn_in['shared_down_w']}
    _x0 = _d['L0_attn_x']
    _d['L0_attn_x'] = jax.random.normal(jax.random.fold_in(jax.random.key(seed), 1), (4, 512, 256), dtype=_x0.dtype)
    del _x0
    return _d

def reference(L0_attn_x, L0_attn_Wq, L0_attn_Wk, L0_attn_Wv, L0_attn_Wo, L0_attn_bo, L0_ffn_W_router, L0_ffn_W_gate, L0_ffn_W_up, L0_ffn_W_down, L0_ffn_sA_gate, L0_ffn_sB_gate, L0_ffn_sA_up, L0_ffn_sB_up, L0_ffn_sA_down, L0_ffn_sB_down, L0_ffn_A_gate, L0_ffn_B_gate, L0_ffn_A_up, L0_ffn_B_up, L0_ffn_A_down, L0_ffn_B_down, L0_ffn_expert_bias, L1_attn_qkv, L1_attn_o_proj, L1_attn_gamma, L1_attn_beta, L1_ffn_router_w, L1_ffn_router_b, L1_ffn_gate_w, L1_ffn_up_w, L1_ffn_down_w, L1_ffn_shared_gate_w, L1_ffn_shared_up_w, L1_ffn_shared_down_w):

    def _L0_attn_ref(x, Wq, Wk, Wv, Wo, bo):
        import jax, jax.numpy as jnp
        import numpy as np
        HEADS = 16
        KV_GROUPS = 4
        SWA_SIZE = 128
        NEG_INF = jnp.float32(-1e+30)
        B, T, E = x.shape
        M = Wq.shape[1]
        D = M // HEADS
        QG = HEADS // KV_GROUPS
        Q = (x @ Wq).reshape(B, T, KV_GROUPS, QG, D)
        K = (x @ Wk).reshape(B, T, KV_GROUPS, D)
        V = (x @ Wv).reshape(B, T, KV_GROUPS, D)
        scores = jnp.einsum('btgqd,bsgd->bgqts', Q, K) / jnp.sqrt(jnp.float32(D))
        i = jnp.arange(T)[:, None]
        j = jnp.arange(T)[None, :]
        allowed = (j <= i) & (i - j < SWA_SIZE)
        scores = jnp.where(allowed[None, None, None], scores, NEG_INF)
        p = jax.nn.softmax(scores, axis=-1)
        att = jnp.einsum('bgqts,bsgd->btgqd', p, V).reshape(B, T, M)
        return att @ Wo + bo

    def _L0_ffn_ref(x, W_router, W_gate, W_up, W_down, sA_gate, sB_gate, sA_up, sB_up, sA_down, sB_down, A_gate, B_gate, A_up, B_up, A_down, B_down, expert_bias):
        import jax, jax.numpy as jnp
        import numpy as np
        B, L, D = (2, 128, 256)
        E, TOP_K, RANK, DFF = (8, 2, 8, 688)

        def _lora(x, A, Bm, scale):
            return x @ A @ Bm * scale

        def _expert_lora(x, A, Bm, w, scale):
            xA = jnp.einsum('bld,edr->bler', x, A)
            xAB = jnp.einsum('bler,erd->bled', xA, Bm) * scale
            return (xAB * w).sum(axis=2)
        scale = 1.0 / RANK
        logits = x @ W_router
        scores = jax.nn.sigmoid(logits)
        biased = scores + expert_bias
        _, topk_idx = jax.lax.top_k(biased, TOP_K)
        topk_scores = jnp.take_along_axis(scores, topk_idx, axis=-1)
        topk_w = topk_scores / (topk_scores.sum(-1, keepdims=True) + 1e-08)
        one_hot = jax.nn.one_hot(topk_idx, E, dtype=x.dtype)
        expert_weights = (one_hot * topk_w[..., None]).sum(axis=2)
        w = expert_weights[..., None]
        gate = x @ W_gate + _lora(x, sA_gate, sB_gate, scale) + _expert_lora(x, A_gate, B_gate, w, scale)
        up = x @ W_up + _lora(x, sA_up, sB_up, scale) + _expert_lora(x, A_up, B_up, w, scale)
        hidden = jax.nn.silu(gate) * up
        out = hidden @ W_down + _lora(hidden, sA_down, sB_down, scale) + _expert_lora(hidden, A_down, B_down, w, scale)
        return out

    def _L1_attn_ref(x, qkv, o_proj, gamma, beta):
        import jax, jax.numpy as jnp
        import numpy as np
        HIDDEN = 256
        KEY = 256
        EPS = 1e-05
        residual = x
        mu = jnp.mean(x, axis=-1, keepdims=True)
        var = jnp.mean((x - mu) ** 2, axis=-1, keepdims=True)
        x_norm = (x - mu) / jnp.sqrt(var + EPS) * gamma + beta
        q = x_norm @ qkv[:, :KEY]
        k = x_norm @ qkv[:, KEY:2 * KEY]
        v = x_norm @ qkv[:, 2 * KEY:]
        scale = 1.0 / jnp.sqrt(jnp.float32(KEY))
        scores = jnp.einsum('bsk,btk->bst', q, k) * scale
        S_len = x.shape[1]
        causal = jnp.tril(jnp.ones((S_len, S_len), dtype=bool))
        scores = jnp.where(causal[None], scores, -jnp.inf)
        attn = jax.nn.softmax(scores, axis=-1)
        out = attn @ v
        out = out @ o_proj
        return out + residual

    def _L1_ffn_ref(x, router_w, router_b, gate_w, up_w, down_w, shared_gate_w, shared_up_w, shared_down_w):
        import jax, jax.numpy as jnp
        import numpy as np
        B, S, H = (1, 64, 256)
        I = 192
        E = 32
        K = 4
        SCALE = 1.8
        b, s, h = x.shape
        xf = x.reshape(-1, h).astype(jnp.float32)
        logits = xf @ router_w.T + router_b
        top_vals, top_idx = jax.lax.top_k(logits, K)
        rw = jax.nn.softmax(top_vals, axis=-1) * SCALE
        combine = jnp.einsum('tke,tk->te', jax.nn.one_hot(top_idx, E, dtype=xf.dtype), rw)
        g = jax.nn.silu(jnp.einsum('th,eih->tei', xf, gate_w))
        u = jnp.einsum('th,eih->tei', xf, up_w)
        routed = jnp.einsum('tei,ehi,te->th', g * u, down_w, combine)
        sg = jax.nn.silu(xf @ shared_gate_w.T)
        su = xf @ shared_up_w.T
        shared = sg * su @ shared_down_w.T
        return (routed + shared).reshape(b, s, h)
    x = L0_attn_x
    xn = _layernorm(x, axis=-1)
    x = x + _L0_attn_ref(xn, L0_attn_Wq, L0_attn_Wk, L0_attn_Wv, L0_attn_Wo, L0_attn_bo) + _L0_ffn_ref(xn, L0_ffn_W_router, L0_ffn_W_gate, L0_ffn_W_up, L0_ffn_W_down, L0_ffn_sA_gate, L0_ffn_sB_gate, L0_ffn_sA_up, L0_ffn_sB_up, L0_ffn_sA_down, L0_ffn_sB_down, L0_ffn_A_gate, L0_ffn_B_gate, L0_ffn_A_up, L0_ffn_B_up, L0_ffn_A_down, L0_ffn_B_down, L0_ffn_expert_bias)
    xn = _layernorm(x, axis=-1)
    x = x + _L1_attn_ref(xn, L1_attn_qkv, L1_attn_o_proj, L1_attn_gamma, L1_attn_beta) + _L1_ffn_ref(xn, L1_ffn_router_w, L1_ffn_router_b, L1_ffn_gate_w, L1_ffn_up_w, L1_ffn_down_w, L1_ffn_shared_gate_w, L1_ffn_shared_up_w, L1_ffn_shared_down_w)
    return x

_drawn_inputs = setup_inputs


def setup_inputs(seed=0):
    import zlib

    import numpy as np

    out = dict(_drawn_inputs(seed))
    spreads = {'L0_attn_bo': (0.0, 0.1),
     'L0_ffn_expert_bias': (0.0, 0.8),
     'L1_attn_gamma': (1.0, 0.6),
     'L1_attn_beta': (0.0, 0.564),
     'L1_ffn_router_b': (0.0, 0.1)}
    factors = {'L0_ffn_W_router': 4.949,
     'L0_ffn_sA_gate': 5.653,
     'L0_ffn_sB_gate': 5.537,
     'L0_ffn_sA_up': 5.132,
     'L0_ffn_sB_up': 6.655,
     'L0_ffn_sA_down': 5.567,
     'L0_ffn_sB_down': 4.869,
     'L0_ffn_A_gate': 5.701,
     'L0_ffn_B_gate': 5.905,
     'L0_ffn_A_up': 7.35,
     'L0_ffn_B_up': 6.863,
     'L0_ffn_A_down': 6.882,
     'L0_ffn_B_down': 6.003}
    for name, (base, spread) in spreads.items():
        noise = np.random.default_rng([zlib.crc32(name.encode()), seed]).standard_normal(out[name].shape)
        drawn = base * np.exp(spread * noise) if base else spread * noise
        out[name] = jnp.asarray(drawn.astype(out[name].dtype))
    for name, factor in factors.items():
        out[name] = (out[name] * factor).astype(out[name].dtype)
    return out
```

```python
from contextlib import ExitStack

import numpy as np
import concourse.bass as bass
from concourse import mybir

ALU = mybir.AluOpType
ACT = mybir.ActivationFunctionType
F32 = mybir.dt.float32
F32R = mybir.dt.float32r
U32 = mybir.dt.uint32
I32 = mybir.dt.int32
AX = mybir.AxisListType


P = 128
B, T, D = 4, 512, 256
NT, KD = T // P, D // P
EPS = 1e-5
HEADS, GROUPS, HD, WINDOW = 16, 4, 16, 128
PAIRS = HEADS // 2
UNITS = PAIRS * NT
Q_SCALE = HD ** -0.5
NEG = -4e30
E0, RANK, DFF = 8, 8, 688
LORA = RANK * (E0 + 1)
MT = -(-DFF // P)
DFF_LAST = DFF - (MT - 1) * P

C_GATE, C_UP, C_WO = 0, DFF, 2 * DFF
C_AG = C_WO + D
C_AU = C_AG + LORA
C_V = C_AU + LORA
C_R0 = C_V + GROUPS * HD
C_Q = C_R0 + E0
C_K = C_Q + D
W0 = C_K + GROUPS * HD
W0S = C_Q
K_ID, K_WIN, K_CAUSAL = 0, P, 6 * P
K_BQ = 7 * P
K_BK, K_MS = K_BQ + 1, K_BQ + 2
K_IOTA = K_BQ + 4
K_EARLIER = K_IOTA + P
NC = K_EARLIER + P


def constants():
    c = np.zeros((P, NC), np.float32)
    q, k = np.arange(P)[:, None], np.arange(2 * P)[None, :]
    c[:, K_ID:K_ID + P] = np.eye(P)
    c[:, K_WIN:K_WIN + 2 * P] = np.where((k > q) & (k <= q + P), 0.0, NEG)
    c[:, K_CAUSAL:K_CAUSAL + P] = np.where(k[:, :P] <= q, 0.0, NEG)
    block = np.arange(P) // 32
    c[:, K_BQ] = block % 2
    c[:, K_BK] = block // 2
    sign = np.array([1.0, -1.0, -1.0, 1.0])[block]
    for s in range(2):
        c[:, K_MS + s] = sign * ((np.arange(P) % 32) // HD == s)
    c[:, K_IOTA:K_IOTA + P] = np.arange(P)
    c[:, K_EARLIER:K_EARLIER + P] = np.arange(P)[:, None] < np.arange(P)
    return c


def product3(pe, out, lhs, rhs, start, stop):
    pe.matmul(out, lhs[0], rhs[0], start=start, stop=False)
    pe.matmul(out, lhs[0], rhs[1], start=False, stop=False)
    return pe.matmul(out, lhs[1], rhs[0], start=False, stop=stop)


def layer0(nc, state, x, w0, wb, wd, vec, const, x1_dram):
    with ExitStack() as ctx:
        def sb(name, shape, dt=F32):
            return ctx.enter_context(nc.sbuf_tensor(name, shape, dt))

        def psum(name, shape):
            return ctx.enter_context(nc.psum_tensor(name, shape, F32))

        def sem(name):
            return ctx.enter_context(nc.semaphore(name))

        w_s = [sb(f"w_{n}", [P, KD, W0S], F32R) for n in ("hi", "lo")]
        wq_s = [sb(f"wq_{n}", [P, KD, PAIRS, 4, 32], F32R) for n in ("hi", "lo")]
        wk_s = [sb(f"wk_{n}", [P, KD, GROUPS, 8, HD], F32R) for n in ("hi", "lo")]
        wb_s = [sb(f"wb_{n}", [LORA, 2 * DFF + D], F32R) for n in ("hi", "lo")]
        wd_s = [sb(f"wd_{n}", [P, MT, D + LORA], F32R) for n in ("hi", "lo")]
        con, mhalf = state["con"], state["mhalf"]
        bo_sb = sb("bo_sb", [P, D])
        eb_sb = sb("eb_sb", [P, E0])
        ident = con[:, K_ID:K_ID + P]

        s_load = [sem(f"s_load{n}") for n in range(8)]
        s_whi = sem("s_whi")
        s_wlo = sem("s_wlo")
        s_mh = sem("s_mh")
        f_ready = [sem(f"f_ready{n}") for n in range(4)]

        with ExitStack() as setup:
            st_w = setup.enter_context(nc.sbuf_tensor("st_w", [P, KD, W0], F32))
            st_b = setup.enter_context(nc.sbuf_tensor("st_b", [LORA, 2 * DFF + D], F32))
            st_d = setup.enter_context(nc.sbuf_tensor("st_d", [P, MT, D + LORA], F32))
            block = setup.enter_context(nc.Block())
            d_last = (slice(0, DFF_LAST), MT - 1)
            d_full = (slice(0, P), slice(0, MT - 1))

            @block.sync
            def _(sp):
                for k in range(KD):
                    sp.dma_start(st_w[:, k, :], w0[k * P:(k + 1) * P, :]).then_inc(s_load[k], 16)
                sp.dma_start(st_d[:, 0:MT - 1, :], wd[0:(MT - 1) * P, :].rearrange("(k p) n -> p k n", p=P))\
                    .then_inc(s_load[2], 16)
                sp.dma_start(st_d[0:DFF_LAST, MT - 1, :], wd[(MT - 1) * P:DFF, :]).then_inc(s_load[3], 16)

            @block.scalar
            def _(act):
                act.dma_start(con[:, :], const).then_inc(s_load[4], 16)
                act.dma_start(st_b[:, :], wb).then_inc(s_load[5], 16)
                act.dma_start(bo_sb[:, :], vec[0:D].partition_broadcast(P)).then_inc(s_load[6], 16)
                act.dma_start(eb_sb[:, :], vec[D:D + E0].partition_broadcast(P)).then_inc(s_load[7], 16)
                for k in range(KD):
                    act.wait_ge(s_load[k], 16)
                    act.activation(w_s[0][:, k, :], st_w[:, k, 0:W0S], ACT.Copy).then_inc(s_whi, 1)
                act.wait_ge(s_load[2], 16)
                act.activation(wd_s[0][d_full], st_d[d_full], ACT.Copy).then_inc(s_whi, 1)
                act.wait_ge(s_load[3], 16)
                act.activation(wd_s[0][d_last], st_d[d_last], ACT.Copy).then_inc(s_whi, 1)
                act.wait_ge(s_load[5], 16)
                act.activation(wb_s[0][:, :], st_b[:, :], ACT.Copy).then_inc(s_whi, 1)
                for n in (4, 6, 7):
                    act.wait_ge(s_load[n], 16)

            @block.gpsimd
            def _(pool):
                pool.memset(mhalf[:, :], -0.5).then_inc(s_mh, 1)
                pool.wait_ge(s_mh, 1)

            @block.vector
            def _(dve):
                def spread(k):
                    q = st_w[:, k, C_Q:C_Q + D].rearrange("p (j o c) -> p j o c", j=PAIRS, o=1)
                    g = st_w[:, k, C_K:W0].rearrange("p (g o c) -> p g o c", g=GROUPS, o=1)
                    return q.broadcast_to([P, PAIRS, 4, 32]), g.broadcast_to([P, GROUPS, 8, HD])

                for k in range(KD):
                    dve.wait_ge(s_load[k], 16)
                    q, g = spread(k)
                    dve.tensor_copy(wq_s[0][:, k], q)
                    dve.tensor_copy(wk_s[0][:, k], g).then_inc(s_whi, 1)
                dve.wait_ge(s_whi, 7)
                for k in range(KD):
                    q, g = spread(k)
                    dve.tensor_tensor(wq_s[1][:, k], q, wq_s[0][:, k].bitcast(F32), ALU.subtract)
                    dve.tensor_tensor(wk_s[1][:, k], g, wk_s[0][:, k].bitcast(F32), ALU.subtract)
                    dve.tensor_tensor(w_s[1][:, k, :], st_w[:, k, 0:W0S], w_s[0][:, k, :].bitcast(F32), ALU.subtract)
                dve.tensor_tensor(wb_s[1][:, :], st_b[:, :], wb_s[0][:, :].bitcast(F32), ALU.subtract)
                for part in (d_full, d_last):
                    dve.tensor_tensor(wd_s[1][part], st_d[part], wd_s[0][part].bitcast(F32), ALU.subtract).then_inc(s_wlo, 1)

        xin = sb("xin", [P, NT, D])
        xb = sb("xb", [P, NT, D])
        xn = sb("xn", [P, NT, D])
        bst = sb("bst", [P, NT, 6])
        mv = sb("mv", [P, NT, 2])
        vpe = sb("vpe", [P, NT])
        rstd = sb("rstd", [P, NT])
        xT = [sb(f"xT_{n}", [P, KD, T], F32R) for n in ("hi", "lo")]
        ex = sb("ex", [P, NT, E0])
        sg = sb("sg", [P, NT, E0])
        bi = sb("bi", [P, NT, E0])
        top = sb("top", [P, NT, 8])
        idx = sb("idx", [P, NT, 8], U32)
        idf = sb("idf", [P, NT, 8])
        hot = sb("hot", [P, 2, NT, E0])
        hs = sb("hs", [P, NT, E0])
        sel = sb("sel", [P, NT, E0])
        ssum = sb("ssum", [P, NT])
        srec = sb("srec", [P, NT])
        wexp = sb("wexp", [P, NT, LORA])
        wexpT = sb("wexpT", [LORA, T])
        kH = sb("kH", [P, T], F32R)
        kT = sb("kT", [P, T])
        kblk = [sb(f"kblk{n}", [P, 2, T], F32R) for n in range(2)]
        qH = sb("qH", [P, 2, T], F32R)
        qs = [sb(f"qs{n}", [P, T], F32R) for n in range(2)]
        vv = sb("vv", [P, NT, GROUPS * HD])
        sc = sb("sc", [P, 3, 2 * 2 * P])
        nm = sb("nm", [P, 3, 2])
        rsum = sb("rsum", [P, 2, NT, 2])
        rrec = sb("rrec", [P, 2, NT, 2])
        pT = sb("pT", [P, 3, 2 * 2 * P])
        att = sb("att", [P, NT, D])
        aT = [sb(f"aT_{n}", [P, KD, T], F32R) for n in ("hi", "lo")]
        tt = sb("tt", [LORA, 2, T])
        tg = [[sb(f"t{m}_{n}", [LORA, T], F32R) for n in ("hi", "lo")] for m in ("gate", "up")]
        tg.append(tg[0])
        th = sb("th", [P, 2, T])
        gg = sb("gg", [P, 2, T])
        hd = sb("hd", [P, 2, T])
        hid = [sb(f"hid_{n}", [P, MT, T], F32R) for n in ("hi", "lo")]

        FB = [psum(f"FB{n}", [P, 512]) for n in range(4)]
        SB = [psum(f"SB{n}", [P, 512]) for n in range(2)]
        TB = psum("TB", [P, 512])
        OB = psum("OB", [P, 512])

        s_x = sem("s_x")
        s_passed = sem("s_passed")
        s_bn, s_ag, s_ve, s_rs, s_xn, s_xb = (sem(n) for n in ("s_bn", "s_ag", "s_ve", "s_rs", "s_xn", "s_xb"))
        s_hi, s_lo = sem("s_hi"), sem("s_lo")
        s_ex, s_rt, s_rw, s_wx, s_wxT, s_v = (sem(n) for n in ("s_ex", "s_rt", "s_rw", "s_wx", "s_wxT", "s_v"))
        s_kH, s_kT, s_kb, s_qH, s_q = (sem(n) for n in ("s_kH", "s_kT", "s_kb", "s_qH", "s_q"))
        s_t, s_thi, s_tlo = sem("s_t"), sem("s_thi"), sem("s_tlo")
        s_tanh, s_gg, s_hd, s_hhi, s_hlo = (sem(n) for n in ("s_tanh", "s_gg", "s_hd", "s_hhi", "s_hlo"))
        s_S, s_m, s_e, s_T, s_ptE, s_ptO, s_PV = (sem(n) for n in ("s_S", "s_m", "s_e", "s_T", "s_ptE", "s_ptO", "s_PV"))
        s_rr, s_at, s_x1, s_out = (sem(n) for n in ("s_rr", "s_at", "s_x1", "s_out"))

        GU = [(n, m) for m in range(MT) for n in ("gate", "up")]
        fill = {0: [("q", 1)], 1: [("k", 1)], 2: [("wx", 0)], 3: [("tin", 0), ("tin", 1)], 4: [("q", 2)], 8: [("q", 3)],
                10: [("k", 2)], 12: [("q", 4)], 16: [("q", 5)], 18: [("k", 3)], 20: [("q", 6)], 24: [("q", 7)]}
        for u, job in zip((5, 6, 7, 9, 11, 13, 15, 17, 21, 23, 26, 28), GU):
            fill[u] = [job]
        jobs = [("xT", 0), ("xT", 1), ("router", 0), ("v", 0), ("k", 0), ("q", 0)]
        for u in sorted(fill):
            jobs += fill[u]
        jobs += [("aT", 0), ("aT", 1), ("tdown", 0), ("y", 0), ("y", 1)]
        USES = len(jobs) // 4
        assert len(jobs) == 4 * USES

        def bank(job):
            n = jobs.index(job)
            return n % 4, n // 4

        def nk(t):
            return 1 if t == 0 else 2

        with ExitStack() as run:
            block = run.enter_context(nc.Block())

            @block.sync
            def _(sp):
                with sp.Fori(0, B) as i:
                    sp.wait_ge(s_xn, i * NT + 1)
                    sp.sem_inc(s_passed, 1)
                    sp.wait_ge(s_xb, i + 1)
                    sp.sem_inc(s_passed, 1)
                    sp.dma_start(xin[:, :, :], x[bass.ds(i, 1)].rearrange("o (t p) d -> p (o t) d", p=P)).then_inc(s_x, 16)
                    for h in range(2):
                        sp.wait_ge(s_x1, i * 2 + h + 3)
                        sp.sem_inc(s_passed, 1)
                        sp.dma_start(x1_dram[bass.ds(i, 1), h * 256:(h + 1) * 256].rearrange("o (t p) d -> p (o t) d", p=P),
                                     xb[:, 2 * h:2 * h + 2, :]).then_inc(s_out, 16)
                sp.wait_ge(s_out, 2 * B * 16 + 16)

            @block.gpsimd
            def _(pool):
                pool.sem_inc(s_xb, 1)
                pool.sem_inc(s_out, 16)
                with pool.Fori(0, B) as i:
                    pool.wait_ge(s_ag, i + 1)
                    pool.sem_inc(s_passed, 1)
                    pool.tensor_scalar(vpe[:, :], mv[:, :, 1], EPS, None, ALU.add).then_inc(s_ve, 1)
                    pool.wait_ge(s_ve, i + 1)
                    pool.tensor_tensor(rstd[:, :], vpe[:, :], mhalf[:, :], ALU.pow).then_inc(s_rs, 1)
                    pool.wait_ge(s_out, i * 32 + 16)
                    pool.tensor_tensor(xb[:, :, :], xin[:, :, :], bo_sb[:, :].unsqueeze(1).broadcast_to([P, NT, D]), ALU.add)\
                        .then_inc(s_xb, 1)
                    for m in range(MT):
                        pool.wait_ge(s_hhi, i * MT + m + 1)
                        r = P if m < MT - 1 else DFF_LAST
                        pool.tensor_tensor(hid[1][0:r, m, :], hd[0:r, m % 2, :], hid[0][0:r, m, :].bitcast(F32), ALU.subtract)\
                            .then_inc(s_hlo, 1)

            @block.scalar
            def _(act):
                def ready(job, i):
                    b, use = bank(job)
                    act.wait_ge(f_ready[b], i * USES + use + 1)
                    return FB[b]

                def high_of(job, i, out):
                    act.activation(out, ready(job, i)[:, :], ACT.Copy).then_inc(s_hi, 1)

                def exp_unit(u, i):
                    j, t = divmod(u, NT)
                    act.wait_ge(s_m, i * UNITS + u + 1)
                    n = nk(t) * P
                    for h in range(2):
                        s = sc[:, u % 3, h * n:(h + 1) * n]
                        last = act.activation(s, s, ACT.Exp, bias=nm[:, u % 3, h:h + 1], scale=-1.0,
                                              accum_out=rsum[:, j % 2, t, h:h + 1])
                    last.then_inc(s_e, 1)

                def copy_pT(u, i):
                    n = 2 * nk(u % NT) * P
                    act.wait_ge(s_T, i * UNITS + u + 1)
                    if u >= 3:
                        act.wait_ge(s_PV, i * UNITS + u - 2)
                    act.activation(pT[:, u % 3, 0:n], TB[:, 0:n], ACT.Copy).then_inc(s_ptE, 1)

                def job_part(job, i):
                    kind, m = job
                    if kind == "k":
                        if m >= 1:
                            act.wait_ge(s_kb, i * GROUPS + m)
                        act.activation(kH[:, :], ready(job, i)[:, :], ACT.Copy).then_inc(s_kH, 1)
                    elif kind == "q":
                        if m >= 2:
                            act.wait_ge(s_q, i * PAIRS + m - 1)
                        act.activation(qH[:, m % 2, :], ready(job, i)[:, :], ACT.Copy).then_inc(s_qH, 1)
                    elif kind == "wx":
                        act.activation(wexpT[:, :], ready(job, i)[0:LORA, :], ACT.Copy).then_inc(s_wxT, 1)
                    elif kind == "tin":
                        act.wait_ge(s_t, i * 3 + m + 1)
                        act.activation(tg[m][0][:, :], tt[:, m, :], ACT.Copy).then_inc(s_thi, 1)
                    elif kind == "gate":
                        if m >= 2:
                            act.wait_ge(s_gg, i * MT + m - 1)
                        act.activation(th[:, m % 2, :], ready(job, i)[:, :], ACT.Tanh, scale=0.5).then_inc(s_tanh, 1)
                    elif kind == "up":
                        act.wait_ge(s_hd, i * MT + m + 1)
                        r = P if m < MT - 1 else DFF_LAST
                        act.activation(hid[0][0:r, m, :], hd[0:r, m % 2, :], ACT.Copy).then_inc(s_hhi, 1)

                with act.Fori(0, B) as i:
                    for k in range(KD):
                        high_of(("xT", k), i, xT[0][:, k, :])
                    act.activation(ex[:, :, :].rearrange("p t e -> p (t e)"), ready(("router", 0), i)[:, 0:NT * E0],
                                        ACT.Exp, scale=-1.0).then_inc(s_ex, 1)
                    act.activation(vv[:, :, :].rearrange("p t e -> p (t e)"), ready(("v", 0), i)[:, 0:NT * GROUPS * HD],
                                        ACT.Copy).then_inc(s_v, 1)
                    job_part(("k", 0), i)
                    job_part(("q", 0), i)
                    for u in range(UNITS + 1):
                        if u < UNITS:
                            exp_unit(u, i)
                        for job in fill.get(u, []):
                            job_part(job, i)
                        if u >= 1 and (u - 1) % 2 == 0:
                            copy_pT(u - 1, i)
                    for k in range(KD):
                        high_of(("aT", k), i, aT[0][:, k, :])
                    act.wait_ge(s_t, i * 3 + 3)
                    act.activation(tg[2][0][:, :], tt[:, 0, :], ACT.Copy).then_inc(s_thi, 1)

            @block.vector
            def _(dve):
                steps = [0]

                def ready(job, i):
                    b, use = bank(job)
                    dve.wait_ge(f_ready[b], i * USES + use + 1)
                    return FB[b]

                def softmax_shift(u, i):
                    t = u % NT
                    n = nk(t) * P
                    mask = con[:, K_WIN:K_WIN + n] if t else con[:, K_CAUSAL:K_CAUSAL + n]
                    dve.wait_ge(s_S, i * UNITS + u + 1)
                    if u >= 3:
                        dve.wait_ge(s_T, i * UNITS + u - 2)
                    dve.sem_inc(s_passed, 1)
                    for h in range(2):
                        last = dve.tensor_tensor_reduce(sc[:, u % 3, h * n:(h + 1) * n], SB[u % 2][:, h * n:(h + 1) * n], mask,
                                                        -Q_SCALE, 3e38, ALU.add, ALU.min, nm[:, u % 3, h:h + 1])
                    last.then_inc(s_m, 1)

                def copy_pT(u, i):
                    n = 2 * nk(u % NT) * P
                    dve.wait_ge(s_T, i * UNITS + u + 1)
                    if u >= 3:
                        dve.wait_ge(s_PV, i * UNITS + u - 2)
                    dve.tensor_copy(pT[:, u % 3, 0:n], TB[:, 0:n]).then_inc(s_ptO, 1)

                def normalise(j, i):
                    dve.wait_ge(s_e, i * UNITS + NT * (j + 1))
                    dve.reciprocal(rrec[:, j % 2], rsum[:, j % 2]).then_inc(s_rr, 1)
                    dve.wait_ge(s_rr, i * PAIRS + j + 1)
                    dve.wait_ge(s_PV, i * UNITS + NT * (j + 1))
                    dve.tensor_tensor(att[:, :, 32 * j:32 * j + 32].rearrange("p t (h d) -> p t h d", h=2),
                                      OB[:, 0:NT * 32].rearrange("p (t h d) -> p t h d", t=NT, h=2),
                                      rrec[:, j % 2].unsqueeze(3).broadcast_to([P, NT, 2, HD]), ALU.mult).then_inc(s_at, 1)

                def low_of(job, i, out, high, count):
                    src = ready(job, i)
                    dve.wait_ge(s_hi, i * 2 * KD + count)
                    dve.tensor_tensor(out, src[:, :], high.bitcast(F32), ALU.subtract).then_inc(s_lo, 1)

                def lora_part(job, slot, n, i):
                    src = ready(job, i)
                    dve.wait_ge(s_wxT, i + 1)
                    dve.tensor_tensor(tt[:, slot, :], src[0:LORA, :], wexpT[:, :], ALU.mult).then_inc(s_t, 1)
                    dve.wait_ge(s_thi, i * 3 + n + 1)
                    dve.tensor_tensor(tg[n][1][:, :], tt[:, slot, :], tg[n][0][:, :].bitcast(F32), ALU.subtract)\
                        .then_inc(s_tlo, 1)

                def job_part(job, i):
                    kind, m = job
                    if kind == "k":
                        src = ready(job, i)
                        dve.wait_ge(s_kH, i * GROUPS + m + 1)
                        dve.scalar_tensor_tensor(kT[:, :], src[:, :], con[:, K_BK:K_BK + 1], kH[:, :].bitcast(F32),
                                                      ALU.mult, ALU.subtract).then_inc(s_kT, 1)
                        dve.wait_ge(s_kT, i * GROUPS + m + 1)
                        if m >= 2:
                            dve.wait_ge(s_S, i * UNITS + 8 * (m - 1))
                        for s in range(2):
                            last = dve.tensor_scalar(kblk[m % 2][:, s, :], kT[:, :], con[:, K_MS + s:K_MS + s + 1], None, ALU.mult)
                        last.then_inc(s_kb, 1)
                    elif kind == "q":
                        src = ready(job, i)
                        dve.wait_ge(s_qH, i * PAIRS + m + 1)
                        if m >= 2:
                            dve.wait_ge(s_S, i * UNITS + NT * (m - 1))
                        dve.scalar_tensor_tensor(qs[m % 2][:, :], src[:, :], con[:, K_BQ:K_BQ + 1],
                                                      qH[:, m % 2, :].bitcast(F32), ALU.mult, ALU.subtract).then_inc(s_q, 1)
                    elif kind == "tin":
                        lora_part(job, m, m, i)
                    elif kind == "gate":
                        src = ready(job, i)
                        dve.wait_ge(s_tanh, i * MT + m + 1)
                        dve.scalar_tensor_tensor(gg[:, m % 2, :], th[:, m % 2, :], 1.0, src[:, :], ALU.add, ALU.mult).then_inc(s_gg, 1)
                    elif kind == "up":
                        src = ready(job, i)
                        if m >= 2:
                            dve.wait_ge(s_hlo, i * MT + m - 1)
                        dve.wait_ge(s_gg, i * MT + m + 1)
                        dve.scalar_tensor_tensor(hd[:, m % 2, :], gg[:, m % 2, :], 0.5, src[:, :], ALU.mult, ALU.mult).then_inc(s_hd, 1)

                def router(i):
                    base = i * 9

                    def link(ins, n):
                        ins.then_inc(s_rt, 1)
                        dve.wait_ge(s_rt, base + n)
                        if n in (3, 4):
                            dve.sem_inc(s_passed, 1)

                    dve.wait_ge(s_ex, i + 1)
                    link(dve.tensor_scalar(ex[:, :, :], ex[:, :, :], 1.0, None, ALU.add), 1)
                    link(dve.reciprocal(sg[:, :, :], ex[:, :, :]), 2)
                    link(dve.tensor_tensor(bi[:, :, :], sg[:, :, :], eb_sb[:, :].unsqueeze(1).broadcast_to([P, NT, E0]), ALU.add), 3)
                    for t in range(NT):
                        last = dve.max(top[:, t, :], bi[:, t, :])
                    link(last, 4)
                    for t in range(NT):
                        last = dve.max_index(idx[:, t, :], top[:, t, :], bi[:, t, :])
                    link(last, 5)
                    iota = con[:, K_IOTA:K_IOTA + E0].unsqueeze(1).broadcast_to([P, NT, E0])
                    link(dve.tensor_copy(idf[:, :, :], idx[:, :, :]), 6)
                    for s in range(2):
                        last = dve.tensor_tensor(hot[:, s], idf[:, :, s:s + 1].broadcast_to([P, NT, E0]), iota, ALU.is_equal)
                    link(last, 7)
                    link(dve.tensor_tensor(hs[:, :, :], hot[:, 0], hot[:, 1], ALU.add), 8)
                    link(dve.tensor_tensor(sel[:, :, :], hs[:, :, :], sg[:, :, :], ALU.mult), 9)

                def router_weights(i):
                    base = i * 3

                    def link(ins, n):
                        ins.then_inc(s_rw, 1)
                        dve.wait_ge(s_rw, base + n)

                    link(dve.tensor_reduce(ssum[:, :], sel[:, :, :], AX.X, ALU.add), 1)
                    link(dve.tensor_scalar(ssum[:, :], ssum[:, :], 1e-8, float(RANK), ALU.add, ALU.mult), 2)
                    link(dve.reciprocal(srec[:, :], ssum[:, :]), 3)
                    dve.memset(wexp[:, :, 0:RANK], 1.0 / RANK)
                    dve.tensor_tensor(wexp[:, :, RANK:LORA].rearrange("p t (e r) -> p t e r", r=RANK),
                                      sel[:, :, :].unsqueeze(3).broadcast_to([P, NT, E0, RANK]),
                                      srec[:, :].unsqueeze(2).unsqueeze(3).broadcast_to([P, NT, E0, RANK]), ALU.mult)\
                        .then_inc(s_wx, 1)

                dve.sem_inc(s_xn, 1)
                dve.sem_inc(s_x1, 1)
                dve.sem_inc(s_x1, 1)
                with dve.Fori(0, B) as i:
                    dve.wait_ge(s_x, i * 16 + 16)
                    for t in range(NT):
                        last = dve.bn_stats(bst[:, t, :], xin[:, t, :])
                    last.then_inc(s_bn, 1)
                    dve.wait_ge(s_bn, i + 1)
                    dve.sem_inc(s_passed, 1)
                    for t in range(NT):
                        last = dve.bn_aggr(mv[:, t, :], bst[:, t, :])
                    last.then_inc(s_ag, 1)
                    dve.wait_ge(s_rs, i + 1)
                    for t in range(NT):
                        dve.tensor_scalar(xn[:, t, :], xin[:, t, :], mv[:, t, 0:1], rstd[:, t:t + 1], ALU.subtract, ALU.mult)\
                            .then_inc(s_xn, 1)
                    for k in range(KD):
                        low_of(("xT", k), i, xT[1][:, k, :], xT[0][:, k, :], k + 1)
                    job_part(("k", 0), i)
                    job_part(("q", 0), i)
                    for u in range(UNITS + 2):
                        if u < UNITS:
                            softmax_shift(u, i)
                        if u == 0:
                            router(i)
                        if u == 1:
                            router_weights(i)
                        for job in fill.get(u, []):
                            job_part(job, i)
                        if 1 <= u <= UNITS and (u - 1) % 2 == 1:
                            copy_pT(u - 1, i)
                        if u >= 2 and (u - 2) % NT == NT - 1:
                            normalise((u - 2) // NT, i)
                    for k in range(KD):
                        low_of(("aT", k), i, aT[1][:, k, :], aT[0][:, k, :], KD + k + 1)
                    lora_part(("tdown", 0), 0, 2, i)
                    for h in range(2):
                        src = ready(("y", h), i)
                        dve.wait_ge(s_xb, i + 2)
                        dve.tensor_tensor(xb[:, 2 * h:2 * h + 2, :].rearrange("p t d -> p (t d)"), src[:, :],
                                               xb[:, 2 * h:2 * h + 2, :].rearrange("p t d -> p (t d)"), ALU.add).then_inc(s_x1, 1)

            @block.tensor
            def _(pe):
                read_by = {"xT": (s_lo, 2 * KD, 1), "aT": (s_lo, 2 * KD, KD + 1), "router": (s_ex, 1, 1), "v": (s_v, 1, 1),
                           "wx": (s_wxT, 1, 1), "k": (s_kT, GROUPS, 1), "q": (s_q, PAIRS, 1), "tin": (s_t, 3, 1),
                           "tdown": (s_t, 3, 3), "gate": (s_gg, MT, 1), "up": (s_hd, MT, 1)}

                def start(job, i):
                    n = jobs.index(job)
                    if n >= 4:
                        kind, m = jobs[n - 4]
                        signal, total, first = read_by[kind]
                        pe.wait_ge(signal, i * total + first + m)
                    elif n >= 2:
                        pe.wait_ge(s_x1, i * 2 + n - 1)
                    return FB[n % 4]

                def done(ins, job):
                    ins.then_inc(f_ready[bank(job)[0]], 1)

                def features(out, first, count, i, extra=None):
                    for k in range(KD):
                        last = product3(pe, out, [w[:, k, first:first + count] for w in w_s], [a[:, k, :] for a in xT],
                                        k == 0, k == KD - 1 and extra is None)
                    if extra is not None:
                        col, t = extra
                        last = product3(pe, out, [w[:, col:col + count] for w in wb_s], [a[:, :] for a in tg[t]], False, True)
                    return last

                def tokens(out, width, first, a):
                    for t in range(NT):
                        for k in range(KD):
                            last = product3(pe, out[:, t * width:(t + 1) * width], [h[:, k, t * P:(t + 1) * P] for h in a],
                                            [w[:, k, first:first + width] for w in w_s], k == 0, k == KD - 1)
                    return last

                def job_part(job, i):
                    kind, m = job
                    out = start(job, i)
                    if kind == "xT":
                        for t in range(NT):
                            pe.wait_ge(s_xn, i * NT + t + 2)
                            last = pe.transpose(out[:, t * P:(t + 1) * P], xn[:, t, m * P:(m + 1) * P], ident)
                    elif kind == "router":
                        pe.wait_ge(s_lo, i * 2 * KD + KD)
                        last = tokens(out, E0, C_R0, xT)
                    elif kind == "v":
                        last = tokens(out, GROUPS * HD, C_V, xT)
                    elif kind == "k":
                        for k in range(KD):
                            last = product3(pe, out[:, :], [w[:, k, m].rearrange("p r c -> p (r c)") for w in wk_s],
                                            [a[:, k, :] for a in xT], k == 0, k == KD - 1)
                    elif kind == "q":
                        for k in range(KD):
                            last = product3(pe, out[:, :], [w[:, k, m].rearrange("p r c -> p (r c)") for w in wq_s],
                                            [a[:, k, :] for a in xT], k == 0, k == KD - 1)
                    elif kind == "wx":
                        pe.wait_ge(s_wx, i + 1)
                        for t in range(NT):
                            last = pe.transpose(out[0:LORA, t * P:(t + 1) * P], wexp[:, t, :], ident)
                    elif kind == "tin":
                        last = features(out[0:LORA, :], C_AU if m else C_AG, LORA, i)
                    elif kind == "gate":
                        if m == 0:
                            pe.wait_ge(s_tlo, i * 3 + 1)
                        last = features(out[:, :], C_GATE + m * P, P, i, (m * P, 0))
                    elif kind == "up":
                        if m == 0:
                            pe.wait_ge(s_tlo, i * 3 + 2)
                        last = features(out[:, :], C_UP + m * P, P, i, (DFF + m * P, 1))
                    elif kind == "aT":
                        pe.wait_ge(s_at, i * PAIRS + PAIRS)
                        for t in range(NT):
                            last = pe.transpose(out[:, t * P:(t + 1) * P], att[:, t, m * P:(m + 1) * P], ident)
                    elif kind == "tdown":
                        pe.wait_ge(s_hlo, i * MT + MT)
                        for k in range(MT):
                            r = P if k < MT - 1 else DFF_LAST
                            last = product3(pe, out[0:LORA, :], [w[0:r, k, D:D + LORA] for w in wd_s],
                                            [h[0:r, k, :] for h in hid], k == 0, k == MT - 1)
                    elif kind == "y":
                        for half in range(2):
                            t = 2 * m + half
                            o, c = out[:, half * D:(half + 1) * D], slice(t * P, (t + 1) * P)
                            for k in range(MT):
                                r = P if k < MT - 1 else DFF_LAST
                                product3(pe, o, [h[0:r, k, c] for h in hid], [w[0:r, k, 0:D] for w in wd_s], k == 0, False)
                            if t == 0:
                                pe.wait_ge(s_lo, i * 2 * KD + 2 * KD)
                            for k in range(KD):
                                product3(pe, o, [a[:, k, c] for a in aT], [w[:, k, C_WO:C_WO + D] for w in w_s], False, False)
                            if t == 0:
                                pe.wait_ge(s_tlo, i * 3 + 3)
                            last = product3(pe, o, [a[:, c] for a in tg[2]], [w[:, 2 * DFF:2 * DFF + D] for w in wb_s],
                                            False, True)
                    done(last, job)

                def scores(u, i):
                    j, t = divmod(u, NT)
                    g = j // 2
                    pe.wait_ge(s_q, i * PAIRS + j + 1)
                    pe.wait_ge(s_kb, i * GROUPS + g + 1)
                    if u >= 2:
                        pe.wait_ge(s_m, i * UNITS + u - 1)
                    first = max(t - 1, 0) * P
                    pe.matmul(SB[u % 2][:, 0:2 * nk(t) * P], qs[j % 2][:, t * P:(t + 1) * P],
                              kblk[g % 2][:, :, first:(t + 1) * P], start=True, stop=True).then_inc(s_S, 1)

                def transposes(u, i):
                    t = u % NT
                    pe.wait_ge(s_e, i * UNITS + u + 1)
                    if u >= 1:
                        v = u - 1
                        pe.wait_ge(s_ptO if v % 2 else s_ptE, i * (UNITS // 2) + v // 2 + 1)
                    for c in range(2 * nk(t)):
                        last = pe.transpose(TB[:, c * P:(c + 1) * P], sc[:, u % 3, c * P:(c + 1) * P], ident)
                    last.then_inc(s_T, 1)

                def values(u, i):
                    j, t = divmod(u, NT)
                    g, n = j // 2, nk(t)
                    if u == 0:
                        pe.wait_ge(s_v, i + 1)
                    pe.wait_ge(s_ptO if u % 2 else s_ptE, i * (UNITS // 2) + u // 2 + 1)
                    if t == 0 and j >= 1:
                        pe.wait_ge(s_at, i * PAIRS + j)
                    for h in range(2):
                        for c in range(n):
                            last = pe.matmul(OB[:, t * 32 + h * HD:t * 32 + (h + 1) * HD],
                                             pT[:, u % 3, (h * n + c) * P:(h * n + c + 1) * P],
                                             vv[:, t + 1 - n + c, g * HD:(g + 1) * HD], start=c == 0, stop=c == n - 1)
                    last.then_inc(s_PV, 1)

                with pe.Fori(0, B) as i:
                    for job in jobs[0:6]:
                        job_part(job, i)
                    for u in range(UNITS + 2):
                        if u < UNITS:
                            scores(u, i)
                        for job in fill.get(u, []):
                            job_part(job, i)
                        if 1 <= u <= UNITS:
                            transposes(u - 1, i)
                        if u >= 2:
                            values(u - 2, i)
                    for job in jobs[-5:]:
                        job_part(job, i)


C1_Q, C1_K, C1_V, C1_O = 0, D, 2 * D, 3 * D
C1_G = 4 * D
E1, TOPK, INNER, ROUTED = 32, 4, 192, 1.8
REST = INNER - P
C1_R = C1_G + 2 * INNER
W1 = C1_R + E1
W1_ALL = W1 + 2
TILES = B * NT
SLOTS = TILES * TOPK + E1
ROWS = SLOTS * P
KEY_SCALE = D ** -0.5


def layer1(nc, state, x1_dram, w1, ws, vec1):
    with ExitStack() as ctx:
        def sb(name, shape, dt=F32):
            return ctx.enter_context(nc.sbuf_tensor(name, shape, dt))

        def sem(name):
            return ctx.enter_context(nc.semaphore(name))

        con, mhalf, xrows, acc = state["con"], state["mhalf"], state["xrows"], state["acc"]
        ident = con[:, K_ID:K_ID + P]
        w_s = [sb(f"v_{n}", [P, KD, W1], F32R) for n in ("hi", "lo")]
        wsd = [sb(f"vs_{n}", [P, KD, D], F32R) for n in ("hi", "lo")]
        gam = sb("gam", [P, KD])
        bet = sb("bet", [P, KD])
        rb_sb = sb("rb_sb", [P, E1])
        s_load = [sem(f"l_load{n}") for n in range(5)]
        s_whi, s_wlo = sem("l_whi"), sem("l_wlo")
        rest = slice(P - REST, P)

        with ExitStack() as setup:
            st_w = setup.enter_context(nc.sbuf_tensor("lst_w", [P, KD, W1_ALL], F32))
            st_s = setup.enter_context(nc.sbuf_tensor("lst_s", [P, KD, D], F32))
            block = setup.enter_context(nc.Block())

            @block.sync
            def _(sp):
                for k in range(KD):
                    sp.dma_start(st_w[:, k, :], w1[k * P:(k + 1) * P, :]).then_inc(s_load[k], 16)
                sp.dma_start(st_s[:, 0, :], ws[0:P, :]).then_inc(s_load[2], 16)
                sp.dma_start(st_s[rest, 1, :], ws[P:INNER, :]).then_inc(s_load[3], 16)
                sp.dma_start(rb_sb[:, :], vec1.partition_broadcast(P)).then_inc(s_load[4], 16)
                sp.wait_ge(s_load[4], 16)

            @block.scalar
            def _(act):
                for k in range(KD):
                    act.wait_ge(s_load[k], 16)
                    act.activation(w_s[0][:, k, :], st_w[:, k, 0:W1], ACT.Copy).then_inc(s_whi, 1)
                act.wait_ge(s_load[2], 16)
                act.activation(wsd[0][:, 0, :], st_s[:, 0, :], ACT.Copy).then_inc(s_whi, 1)
                act.wait_ge(s_load[3], 16)
                act.activation(wsd[0][rest, 1, :], st_s[rest, 1, :], ACT.Copy).then_inc(s_whi, 1)

            @block.vector
            def _(dve):
                for k in range(KD):
                    dve.wait_ge(s_whi, k + 1)
                    dve.tensor_copy(gam[:, k:k + 1], st_w[:, k, W1:W1 + 1])
                    dve.tensor_copy(bet[:, k:k + 1], st_w[:, k, W1 + 1:W1 + 2])
                    dve.tensor_tensor(w_s[1][:, k, :], st_w[:, k, 0:W1], w_s[0][:, k, :].bitcast(F32), ALU.subtract)
                dve.wait_ge(s_whi, 4)
                dve.tensor_tensor(wsd[1][:, 0, :], st_s[:, 0, :], wsd[0][:, 0, :].bitcast(F32), ALU.subtract)
                dve.tensor_tensor(wsd[1][rest, 1, :], st_s[rest, 1, :], wsd[0][rest, 1, :].bitcast(F32), ALU.subtract)\
                    .then_inc(s_wlo, 1)
                dve.wait_ge(s_wlo, 1)

        x1 = sb("l_x1", [P, NT, D])
        xn = sb("l_xn", [P, NT, D])
        z = sb("l_z", [P, NT, D])
        bst = sb("l_bst", [P, 2, NT, 6])
        mv = sb("l_mv", [P, 2, NT, 2])
        vpe = sb("l_vpe", [P, 2, NT])
        rstd = sb("l_rstd", [P, 2, NT])
        xT = [sb(f"l_xT_{n}", [P, KD, T], F32R) for n in ("hi", "lo")]
        zw = sb("l_zw", [P, KD, T])
        zT = [sb(f"l_zT_{n}", [P, KD, T], F32R) for n in ("hi", "lo")]
        qT = [sb(f"l_qT_{n}", [P, KD, T], F32R) for n in ("hi", "lo")]
        kT = [sb(f"l_kT_{n}", [P, KD, T], F32R) for n in ("hi", "lo")]
        vT = [sb(f"l_v_{n}", [P, NT, D], F32R) for n in ("hi", "lo")]
        sc = sb("l_sc", [P, NT, T])
        nm = sb("l_nm", [P, NT])
        rsum = sb("l_rsum", [P, NT])
        rrec = sb("l_rrec", [P, NT])
        pT = [sb(f"l_pT_{n}", [P, NT, T], F32R) for n in ("hi", "lo")]
        oT = [sb(f"l_oT_{n}", [P, KD, T], F32R) for n in ("hi", "lo")]
        th = sb("l_th", [P, KD, T])
        g1 = sb("l_g1", [P, T])
        gg = sb("l_gg", [P, KD, T])
        hw = sb("l_hw", [P, KD, T])
        hT = [sb(f"l_h_{n}", [P, KD, T], F32R) for n in ("hi", "lo")]
        lg = sb("l_lg", [P, NT, E1])
        top = sb("l_top", [P, NT, 8])
        idx = sb("l_idx", [P, NT, 8], U32)
        ev = sb("l_ev", [P, NT, TOPK])
        es = sb("l_es", [P, NT])
        er = sb("l_er", [P, NT])
        rel = sb("l_rel", [P, NT, TOPK])
        ef = sb("l_ef", [P, NT, TOPK])
        hot = sb("l_hot", [P, NT, E1, TOPK])
        accb = sb("l_accb", [P, NT, D])

        FB = [ctx.enter_context(nc.psum_tensor(f"L{n}", [P, 512], F32)) for n in range(8)]
        f_ready = [sem(f"l_ready{n}") for n in range(8)]
        names = ("s_x", "s_bn", "s_ag", "s_ve", "s_rs", "s_xn", "s_z", "s_accb", "s_hi", "s_lo", "s_zw", "s_zhi", "s_zlo", "s_dc",
                 "s_ev", "s_m", "s_e", "s_rr", "s_norm", "s_th", "s_g1", "s_gg", "s_hw", "s_hhi", "s_hlo", "s_y", "s_row",
                 "s_passed")
        S = {n: sem("l_" + n) for n in names}

        jobs = [("x", 0), ("x", 1), ("z", 0), ("z", 1), ("router", 0), ("q", 0), ("q", 1), ("k", 0), ("k", 1), ("s", 0), ("v", 0),
                ("s", 1), ("v", 1), ("s", 2), ("up", 0), ("s", 3), ("up", 1), ("p", 0), ("p", 1), ("up", 2), ("p", 2), ("p", 3),
                ("o", 0), ("o", 1), ("y", 0), ("y", 1)]
        uses = [len(range(n, len(jobs), 8)) for n in range(8)]
        split = [("x", 0), ("x", 1), ("q", 0), ("q", 1), ("k", 0), ("k", 1), ("v", 0), ("v", 1), ("p", 0), ("p", 1), ("p", 2),
                 ("p", 3), ("o", 0), ("o", 1)]

        def ready(eng, job, i):
            n = jobs.index(job)
            eng.wait_ge(f_ready[n % 8], i * uses[n % 8] + n // 8 + 1)
            return FB[n % 8]

        def parts(job):
            kind, m = job
            if kind in ("x", "q", "k", "o"):
                return [a[:, m, :] for a in {"x": xT, "q": qT, "k": kT, "o": oT}[kind]], lambda bank: bank[:, :]
            if kind == "v":
                return [a[:, 2 * m:2 * m + 2, :] for a in vT], lambda bank: bank[:, :].rearrange("p (t d) -> p t d", t=2)
            return ([a[:, 0:m + 1, m * P:(m + 1) * P] for a in pT],
                    lambda bank: bank[:, 0:(m + 1) * P].rearrange("p (c q) -> p c q", c=m + 1))

        with ExitStack() as run:
            block = run.enter_context(nc.Block())

            @block.sync
            def _(sp):
                sp.wait_ge(S["s_row"], 1)
                for c in range(state["fills"]):
                    sp.dma_start(state["rows_dram"].rearrange("(c p r) d -> c p (r d)", c=state["fills"], p=P)[c],
                                 state["zeros"][:, :]).then_inc(state["s_zero"], 16)
                with sp.Fori(0, B) as i:
                    sp.wait_ge(S["s_accb"], i + 1)
                    sp.sem_inc(S["s_passed"], 1)
                    sp.dma_start(x1[:, :, :], x1_dram[bass.ds(i, 1)].rearrange("o (t p) d -> p (o t) d", p=P)).then_inc(S["s_x"], 16)

            @block.gpsimd
            def _(pool):
                pool.memset(state["zeros"][:, :], 0.0).then_inc(S["s_row"], 1)
                pool.sem_inc(S["s_accb"], 1)
                with pool.Fori(0, B) as i:
                    for n in range(2):
                        pool.wait_ge(S["s_ag"], i * 2 + n + 1)
                        pool.sem_inc(S["s_passed"], 1)
                        pool.tensor_scalar(vpe[:, n, :], mv[:, n, :, 1], EPS, None, ALU.add).then_inc(S["s_ve"], 1)
                        pool.wait_ge(S["s_ve"], i * 2 + n + 1)
                        pool.tensor_tensor(rstd[:, n, :], vpe[:, n, :], mhalf[:, :], ALU.pow).then_inc(S["s_rs"], 1)
                        if n == 0:
                            pool.wait_ge(S["s_xn"], i + 1)
                            pool.tensor_tensor(accb[:, :, :], x1[:, :, :], xn[:, :, :], ALU.add).then_inc(S["s_accb"], 1)
                            pool.tensor_copy(xrows[:, bass.ds(i * NT, NT), :], xn[:, :, :]).then_inc(S["s_row"], 1)
                    for k in range(KD):
                        pool.wait_ge(S["s_zhi"], i * KD + k + 1)
                        pool.tensor_tensor(zT[1][:, k, :], zw[:, k, :], zT[0][:, k, :].bitcast(F32), ALU.subtract)\
                            .then_inc(S["s_zlo"], 1)
                    for k in range(KD):
                        r = slice(0, P) if k == 0 else rest
                        pool.wait_ge(S["s_hhi"], i * KD + k + 1)
                        pool.tensor_tensor(hT[1][r, k, :], hw[r, k, :], hT[0][r, k, :].bitcast(F32), ALU.subtract)\
                            .then_inc(S["s_hlo"], 1)
                        pool.wait_ge(S["s_hlo"], i * KD + k + 1)

            @block.scalar
            def _(act):
                def high(job, i):
                    bank = ready(act, job, i)
                    (out, _), view = parts(job)
                    act.activation(out, view(bank), ACT.Copy).then_inc(S["s_hi"], 1)

                def exp_rows(t, i):
                    act.wait_ge(S["s_m"], i * NT + t + 1)
                    s = sc[:, t, 0:(t + 1) * P]
                    act.activation(s, s, ACT.Exp, bias=nm[:, t:t + 1], scale=-1.0, accum_out=rsum[:, t:t + 1])\
                        .then_inc(S["s_e"], 1)

                with act.Fori(0, B) as i:
                    high(("x", 0), i)
                    high(("x", 1), i)
                    for k in range(KD):
                        act.wait_ge(S["s_zw"], i * KD + k + 1)
                        act.activation(zT[0][:, k, :], zw[:, k, :], ACT.Copy).then_inc(S["s_zhi"], 1)
                    for job in (("q", 0), ("q", 1), ("k", 0), ("k", 1)):
                        high(job, i)
                    act.wait_ge(S["s_dc"], i * 8 + 4)
                    act.activation(ev[:, :, :], rel[:, :, :], ACT.Exp).then_inc(S["s_ev"], 1)
                    exp_rows(0, i)
                    high(("v", 0), i)
                    exp_rows(1, i)
                    high(("v", 1), i)
                    exp_rows(2, i)
                    bank = ready(act, ("up", 0), i)
                    act.activation(th[:, 0, :], bank[:, :], ACT.Tanh, scale=0.5).then_inc(S["s_th"], 1)
                    exp_rows(3, i)
                    bank = ready(act, ("up", 1), i)
                    act.activation(th[rest, 1, :], bank[0:REST, :], ACT.Tanh, scale=0.5).then_inc(S["s_th"], 1)
                    act.activation(g1[rest, :], bank[0:REST, :], ACT.Copy).then_inc(S["s_g1"], 1)
                    high(("p", 0), i)
                    high(("p", 1), i)
                    for k in range(KD):
                        r = slice(0, P) if k == 0 else rest
                        act.wait_ge(S["s_hw"], i * KD + k + 1)
                        act.activation(hT[0][r, k, :], hw[r, k, :], ACT.Copy).then_inc(S["s_hhi"], 1)
                    for job in (("p", 2), ("p", 3), ("o", 0), ("o", 1)):
                        high(job, i)

            @block.vector
            def _(dve):
                def low(job, i):
                    bank = ready(dve, job, i)
                    (hi, out), view = parts(job)
                    dve.wait_ge(S["s_hi"], i * len(split) + split.index(job) + 1)
                    dve.tensor_tensor(out, view(bank), hi.bitcast(F32), ALU.subtract).then_inc(S["s_lo"], 1)

                def norm(n, src, out, signal, i):
                    for t in range(NT):
                        last = dve.bn_stats(bst[:, n, t, :], src[:, t, :])
                    last.then_inc(S["s_bn"], 1)
                    dve.wait_ge(S["s_bn"], i * 2 + n + 1)
                    dve.sem_inc(S["s_passed"], 1)
                    for t in range(NT):
                        last = dve.bn_aggr(mv[:, n, t, :], bst[:, n, t, :])
                    last.then_inc(S["s_ag"], 1)
                    dve.wait_ge(S["s_rs"], i * 2 + n + 1)
                    for t in range(NT):
                        last = dve.tensor_scalar(out[:, t, :], src[:, t, :], mv[:, n, t, 0:1], rstd[:, n, t:t + 1],
                                                 ALU.subtract, ALU.mult)
                    last.then_inc(S[signal], 1)

                def shift(t, i):
                    bank = ready(dve, ("s", t), i)
                    dve.sem_inc(S["s_passed"], 1)
                    n = (t + 1) * P
                    dve.tensor_tensor_reduce(sc[:, t, 0:n], bank[:, 0:n], con[:, K_CAUSAL + P - n:K_CAUSAL + P],
                                             -KEY_SCALE, 3e38, ALU.add, ALU.min, nm[:, t:t + 1]).then_inc(S["s_m"], 1)

                def normalise(t, i):
                    dve.wait_ge(S["s_e"], i * NT + t + 1)
                    dve.reciprocal(rrec[:, t:t + 1], rsum[:, t:t + 1]).then_inc(S["s_rr"], 1)
                    dve.wait_ge(S["s_rr"], i * NT + t + 1)
                    s = sc[:, t, 0:(t + 1) * P]
                    dve.tensor_scalar(s, s, rrec[:, t:t + 1], None, ALU.mult).then_inc(S["s_norm"], 1)

                def chain(ins, n, i):
                    ins.then_inc(S["s_dc"], 1)
                    dve.wait_ge(S["s_dc"], i * 8 + n)

                def router(i):
                    bank = ready(dve, ("router", 0), i)
                    chain(dve.tensor_tensor(lg[:, :, :], bank[:, 0:NT * E1].rearrange("p (t e) -> p t e", t=NT),
                                            rb_sb[:, :].unsqueeze(1).broadcast_to([P, NT, E1]), ALU.add), 1, i)
                    dve.sem_inc(S["s_passed"], 1)
                    for t in range(NT):
                        last = dve.max(top[:, t, :], lg[:, t, :])
                    chain(last, 2, i)
                    dve.sem_inc(S["s_passed"], 1)
                    for t in range(NT):
                        last = dve.max_index(idx[:, t, :], top[:, t, :], lg[:, t, :])
                    chain(last, 3, i)
                    chain(dve.tensor_tensor(rel[:, :, :], top[:, :, 0:TOPK], top[:, :, 0:1].broadcast_to([P, NT, TOPK]),
                                            ALU.subtract), 4, i)
                    chain(dve.tensor_copy(ef[:, :, :], idx[:, :, 0:TOPK]), 5, i)
                    dve.tensor_copy(state["choice"][:, bass.ds(i * NT, NT), :], ef[:, :, :])
                    chain(dve.tensor_tensor(hot[:, :, :, :], ef[:, :, :].unsqueeze(2).broadcast_to([P, NT, E1, TOPK]),
                                            con[:, K_IOTA:K_IOTA + E1].unsqueeze(1).unsqueeze(3)
                                            .broadcast_to([P, NT, E1, TOPK]), ALU.is_equal), 6, i)
                    dve.tensor_reduce(state["chosen"][:, bass.ds(i * NT, NT), :], hot[:, :, :, :], AX.X, ALU.add)

                def shares(i):
                    dve.wait_ge(S["s_ev"], i + 1)
                    chain(dve.tensor_reduce(es[:, :], ev[:, :, :], AX.X, ALU.add), 7, i)
                    chain(dve.reciprocal(er[:, :], es[:, :]), 8, i)
                    dve.scalar_tensor_tensor(state["share"][:, bass.ds(i * NT, NT), :], ev[:, :, :], ROUTED,
                                             er[:, :].unsqueeze(2).broadcast_to([P, NT, TOPK]), ALU.mult, ALU.mult)

                with dve.Fori(0, B) as i:
                    dve.wait_ge(S["s_x"], i * 16 + 16)
                    norm(0, x1, xn, "s_xn", i)
                    dve.wait_ge(S["s_xn"], i + 1)
                    norm(1, xn, z, "s_z", i)
                    low(("x", 0), i)
                    low(("x", 1), i)
                    for k in range(KD):
                        bank = ready(dve, ("z", k), i)
                        dve.tensor_scalar(zw[:, k, :], bank[:, :], gam[:, k:k + 1], bet[:, k:k + 1], ALU.mult, ALU.add)\
                            .then_inc(S["s_zw"], 1)
                    router(i)
                    for job in (("q", 0), ("q", 1), ("k", 0), ("k", 1)):
                        low(job, i)
                    shift(0, i)
                    low(("v", 0), i)
                    normalise(0, i)
                    shift(1, i)
                    low(("v", 1), i)
                    normalise(1, i)
                    shares(i)
                    shift(2, i)
                    bank0 = ready(dve, ("up", 0), i)
                    dve.wait_ge(S["s_th"], i * 2 + 1)
                    dve.scalar_tensor_tensor(gg[:, 0, :], th[:, 0, :], 1.0, bank0[:, :], ALU.add, ALU.mult).then_inc(S["s_gg"], 1)
                    normalise(2, i)
                    shift(3, i)
                    low(("p", 0), i)
                    low(("p", 1), i)
                    bank1 = ready(dve, ("up", 1), i)
                    dve.wait_ge(S["s_g1"], i + 1)
                    dve.scalar_tensor_tensor(gg[rest, 1, :], th[rest, 1, :], 1.0, g1[rest, :], ALU.add, ALU.mult).then_inc(S["s_gg"], 1)
                    bank2 = ready(dve, ("up", 2), i)
                    dve.wait_ge(S["s_gg"], i * 2 + 2)
                    dve.scalar_tensor_tensor(hw[:, 0, :], gg[:, 0, :], 0.5, bank2[:, :], ALU.mult, ALU.mult).then_inc(S["s_hw"], 1)
                    dve.scalar_tensor_tensor(hw[rest, 1, :], gg[rest, 1, :], 0.5, bank1[rest, :], ALU.mult, ALU.mult)\
                        .then_inc(S["s_hw"], 1)
                    normalise(3, i)
                    for job in (("p", 2), ("p", 3), ("o", 0), ("o", 1)):
                        low(job, i)
                    for h in range(2):
                        bank = ready(dve, ("y", h), i)
                        dve.wait_ge(S["s_accb"], i + 2)
                        dve.tensor_tensor(acc[:, bass.ds(i * NT + 2 * h, 2), :], bank[:, :].rearrange("p (t d) -> p t d", t=2),
                                          accb[:, 2 * h:2 * h + 2, :], ALU.add).then_inc(S["s_y"], 1)

            @block.tensor
            def _(pe):
                read_by = {"z": (S["s_zw"], KD, 1), "router": (S["s_dc"], 8, 1), "s": (S["s_m"], NT, 1)}

                def start(job, i):
                    n = jobs.index(job)
                    if n >= 8:
                        was, m = jobs[n - 8]
                        if (was, m) in split:
                            pe.wait_ge(S["s_lo"], i * len(split) + split.index((was, m)) + 1)
                        elif was == "up":
                            signal, own = ((S["s_gg"], 1), (S["s_hw"], 2), (S["s_hw"], 1))[m]
                            pe.wait_ge(signal, i * 2 + own)
                        else:
                            signal, total, first = read_by[was]
                            pe.wait_ge(signal, i * total + first + m)
                    return FB[n % 8]

                def parts_ready(job, i):
                    pe.wait_ge(S["s_lo"], i * len(split) + split.index(job) + 1)

                def job_part(job, i):
                    kind, m = job
                    out = start(job, i)
                    if kind in ("x", "z"):
                        pe.wait_ge(S["s_xn" if kind == "x" else "s_z"], i + 1)
                        src = xn if kind == "x" else z
                        for t in range(NT):
                            last = pe.transpose(out[:, t * P:(t + 1) * P], src[:, t, m * P:(m + 1) * P], ident)
                    elif kind == "router":
                        parts_ready(("x", 1), i)
                        for t in range(NT):
                            for k in range(KD):
                                last = product3(pe, out[:, t * E1:(t + 1) * E1], [a[:, k, t * P:(t + 1) * P] for a in xT],
                                                [w[:, k, C1_R:C1_R + E1] for w in w_s], k == 0, k == KD - 1)
                    elif kind in ("q", "k"):
                        pe.wait_ge(S["s_zlo"], i * KD + KD)
                        c = (C1_Q if kind == "q" else C1_K) + m * P
                        for k in range(KD):
                            last = product3(pe, out[:, :], [w[:, k, c:c + P] for w in w_s], [a[:, k, :] for a in zT],
                                            k == 0, k == KD - 1)
                    elif kind == "v":
                        for half in range(2):
                            t = 2 * m + half
                            for k in range(KD):
                                last = product3(pe, out[:, half * D:(half + 1) * D], [a[:, k, t * P:(t + 1) * P] for a in zT],
                                                [w[:, k, C1_V:C1_V + D] for w in w_s], k == 0, k == KD - 1)
                    elif kind == "up":
                        c = C1_G + m * P
                        for k in range(KD):
                            last = product3(pe, out[:, :], [w[:, k, c:c + P] for w in w_s], [a[:, k, :] for a in xT],
                                            k == 0, k == KD - 1)
                    elif kind == "s":
                        parts_ready(("k", 1), i)
                        for k in range(KD):
                            last = product3(pe, out[:, 0:(m + 1) * P], [a[:, k, m * P:(m + 1) * P] for a in qT],
                                            [a[:, k, 0:(m + 1) * P] for a in kT], k == 0, k == KD - 1)
                    elif kind == "p":
                        pe.wait_ge(S["s_norm"], i * NT + m + 1)
                        for c in range(m + 1):
                            last = pe.transpose(out[:, c * P:(c + 1) * P], sc[:, m, c * P:(c + 1) * P], ident)
                    elif kind == "o":
                        parts_ready(("p", 3), i)
                        for c in range(NT):
                            last = product3(pe, out[:, c * P:T], [a[:, c, m * P:(m + 1) * P] for a in vT],
                                            [a[:, c, c * P:T] for a in pT], c == 0, c == NT - 1)
                    elif kind == "y":
                        pe.wait_ge(S["s_hlo"], i * KD + KD)
                        for half in range(2):
                            t = 2 * m + half
                            o, c = out[:, half * D:(half + 1) * D], slice(t * P, (t + 1) * P)
                            for k in range(KD):
                                r = slice(0, P) if k == 0 else rest
                                product3(pe, o, [a[r, k, c] for a in hT], [w[r, k, :] for w in wsd], k == 0, False)
                            parts_ready(("o", 1), i)
                            for k in range(KD):
                                last = product3(pe, o, [a[:, k, c] for a in oT], [w[:, k, C1_O:C1_O + D] for w in w_s],
                                                False, k == KD - 1)
                    last.then_inc(f_ready[jobs.index(job) % 8], 1)

                with pe.Fori(0, B) as i:
                    for job in jobs:
                        job_part(job, i)


RING = 4
STEP = 4
WE = KD * 2 * INNER + KD * D
FILL = 8


def dispatch(nc, state):
    with ExitStack() as ctx:
        def sb(name, shape, dt=F32):
            return ctx.enter_context(nc.sbuf_tensor("d_" + name, shape, dt))

        con = state["con"]
        bf = mybir.dt.bfloat16
        chosen = sb("chosen", [P, TILES * E1], bf)
        earlier = sb("earlier", [P, P], bf)
        ones = sb("ones", [P, P], bf)
        cnt = sb("cnt", [P, E1])
        full = sb("full", [P, E1, TILES])
        zero = sb("zero", [P, E1])
        til = sb("til", [P, E1])
        incl = sb("incl", [P, E1])
        base = sb("base", [P, E1])
        rank = sb("rank", [P, TILES, E1])
        hit = sb("hit", [P, TOPK, TILES, E1])
        pos = sb("pos", [P, TOPK, TILES])
        past = sb("past", [1, SLOTS, E1])
        owner = sb("owner", [1, SLOTS])
        R = ctx.enter_context(nc.psum_tensor("d_rank_bank", [P, TILES * E1], F32))
        N = ctx.enter_context(nc.psum_tensor("d_count_bank", [P, 512], F32))
        s_b, s_r, s_c, s_n = (ctx.enter_context(nc.semaphore(n)) for n in ("d_cast", "d_rank_s", "d_chain", "d_count_s"))
        with nc.Block() as block:
            @block.tensor
            def _(pe):
                pe.wait_ge(s_b, 3)
                for t in range(TILES):
                    last = pe.matmul(N[:, 0:E1], ones[:, :], chosen[:, t * E1:(t + 1) * E1], start=t == 0, stop=t == TILES - 1)
                last.then_inc(s_n, 1)
                pe.matmul(R[:, :], earlier[:, :], chosen[:, :], start=True, stop=False)
                for t in range(1, TILES):
                    last = pe.matmul(R[:, t * E1:], ones[:, :], chosen[:, 0:(TILES - t) * E1], start=False, stop=t == TILES - 1)
                last.then_inc(s_r, 1)

            @block.vector
            def _(dve):
                n = [0]

                def chain(ins):
                    n[0] += 1
                    ins.then_inc(s_c, 1)
                    dve.wait_ge(s_c, n[0])

                dve.tensor_copy(chosen[:, :], state["chosen"][:, :, :].rearrange("p t e -> p (t e)")).then_inc(s_b, 1)
                dve.tensor_copy(earlier[:, :], con[:, K_EARLIER:K_EARLIER + P]).then_inc(s_b, 1)
                dve.memset(ones[:, :], 1.0).then_inc(s_b, 1)
                chain(dve.memset(zero[:, :], 0.0))
                dve.wait_ge(s_n, 1)
                chain(dve.tensor_scalar(cnt[:, :], N[:, 0:E1], 1.0 / P, None, ALU.mult))
                chain(dve.tensor_tensor(full[:, :, :], cnt[:, :].unsqueeze(2).broadcast_to([P, E1, TILES]),
                                        con[:, K_IOTA:K_IOTA + TILES].unsqueeze(1).broadcast_to([P, E1, TILES]), ALU.is_gt))
                chain(dve.tensor_reduce(til[:, :], full[:, :, :], AX.X, ALU.add))
                chain(dve.tensor_tensor_scan(incl[:, :], til[:, :], zero[:, :], 0.0, ALU.add, ALU.add))
                chain(dve.tensor_tensor(base[:, :], incl[:, :], til[:, :], ALU.subtract))
                dve.wait_ge(s_r, 1)
                chain(dve.scalar_tensor_tensor(rank[:, :, :], base[:, :].unsqueeze(1).broadcast_to([P, TILES, E1]), float(P),
                                               R[:, :].rearrange("p (t e) -> p t e", t=TILES), ALU.mult, ALU.add))
                for k in range(TOPK):
                    last = dve.tensor_tensor(hit[:, k], state["choice"][:, :, k:k + 1].broadcast_to([P, TILES, E1]),
                                             con[:, K_IOTA:K_IOTA + E1].unsqueeze(1).broadcast_to([P, TILES, E1]), ALU.is_equal)
                chain(last)
                for k in range(TOPK):
                    last = dve.tensor_tensor(hit[:, k], hit[:, k], rank[:, :, :], ALU.mult)
                chain(last)
                for k in range(TOPK):
                    last = dve.tensor_reduce(pos[:, k, :], hit[:, k], AX.X, ALU.add)
                chain(last)
                chain(dve.tensor_copy(state["pos"][:, :, :], pos[:, :, :]))
                chain(dve.tensor_tensor(past[:, :, :], con[0:1, K_IOTA:K_IOTA + SLOTS].unsqueeze(2).broadcast_to([1, SLOTS, E1]),
                                        incl[0:1, :].unsqueeze(1).broadcast_to([1, SLOTS, E1]), ALU.is_ge))
                chain(dve.tensor_reduce(owner[:, :], past[:, :, :], AX.X, ALU.add))
                chain(dve.tensor_scalar(state["owner"][:, :], owner[:, :], E1 - 1.0, None, ALU.min))
                chain(dve.tensor_scalar(state["place"][:, :], state["owner"][:, :], RING - 1, None, ALU.bitwise_and))
                chain(dve.tensor_copy(state["ends"][:, :], incl[0:1, :]))


def experts(nc, state, wg, wdn, rows_dram, y_dram, out):
    with ExitStack() as ctx:
        def sb(name, shape, dt=F32):
            return ctx.enter_context(nc.sbuf_tensor("e_" + name, shape, dt))

        def sem(name):
            return ctx.enter_context(nc.semaphore("e_" + name))

        con, xrows, acc, pos = state["con"], state["xrows"], state["acc"], state["pos"]
        ident = con[:, K_ID:K_ID + P]
        GU = KD * 2 * INNER
        s_scat = sem("scat")
        with nc.Block() as block:
            @block.gpsimd
            def _(pool):
                pool.wait_ge(state["s_zero"], state["fills"] * 16)
                for t in range(TILES):
                    for k in range(TOPK):
                        pool.indirect_dma_start(out=rows_dram, out_offset=bass.IndirectOffsetOnAxis(pos[:, k, t:t + 1], 0),
                                                in_=xrows[:, t, :], in_offset=None).then_inc(s_scat, 16)
                pool.wait_ge(s_scat, TILES * TOPK * 16)

        with ExitStack() as run:
            def rb(name, shape, dt=F32):
                return run.enter_context(nc.sbuf_tensor("e_" + name, shape, dt))

            stage = rb("stage", [P, RING, WE])
            ring = [rb(f"ring_{n}", [P, RING, WE], F32R) for n in ("hi", "lo")]
            xs = rb("xs", [P, STEP, D])
            xT = [rb(f"xT_{n}", [P, 2, D], F32R) for n in ("hi", "lo")]
            th = rb("th", [P, 2, INNER])
            gg = rb("gg", [P, 2, INNER])
            hh = rb("hh", [P, 2, INNER])
            hT = [rb(f"hT_{n}", [P, 2, 2 * P], F32R) for n in ("hi", "lo")]
            ys = rb("ys", [P, STEP, D])
            XB, GB, HB, YB = ([run.enter_context(nc.psum_tensor(f"e_{n}{b}", [P, 512], F32)) for b in range(2)]
                              for n in "XGHY")
            s_wd = [sem(f"wd{n}") for n in range(RING)]
            s_xs = [sem(f"xs{n}") for n in range(STEP)]
            s_ys = [sem(f"ys{n}") for n in range(STEP)]
            (s_staged, s_whi, s_wlo, s_xt, s_xhi, s_xlo, s_gu, s_th, s_gg, s_hh, s_ht, s_hhi, s_hlo, s_y, s_yc, s_passed) = (
                sem(n) for n in ("staged", "whi", "wlo", "xt", "xhi", "xlo", "gu", "th", "gg", "hh", "ht", "hhi", "hlo", "y",
                                 "yc", "passed"))
            block = run.enter_context(nc.Block())

            def steps(eng, step):
                for u in range(STEP):
                    step(0, u)
                with eng.Fori(1, SLOTS // STEP) as i:
                    for u in range(STEP):
                        step(i * STEP, u)

            @block.sync
            def _(sp):
                sp.sem_inc(s_wlo, 1)

                def load(e, r):
                    w = stage[:, r, 0:GU].rearrange("p (k n) -> p k n", k=KD)
                    sp.dma_start(w, wg[bass.ds(e, 1)].rearrange("o (k p) n -> p (o k) n", p=P)).then_inc(s_wd[r], 16)
                    sp.dma_start(stage[:, r, GU:GU + D], wdn[bass.ds(e, 1), 0:P].rearrange("o p n -> (o p) n")).then_inc(s_wd[r], 16)
                    sp.dma_start(stage[0:REST, r, GU + D:WE], wdn[bass.ds(e, 1), P:INNER].rearrange("o p n -> (o p) n"))\
                        .then_inc(s_wd[r], 16)

                for r in range(RING):
                    load(r, r)
                with sp.Fori(1, E1 // RING) as i:
                    for r in range(RING):
                        sp.wait_ge(s_wlo, i * RING + r - RING + 2)
                        sp.sem_inc(s_passed, 1)
                        load(i * RING + r, r)

            @block.gpsimd
            def _(pool):
                pool.sem_inc(s_y, 1)
                pool.memset(stage[REST:P, :, GU + D:WE], 0.0).then_inc(s_staged, 1)
                pool.wait_ge(s_staged, 1)

                def split(i, r, first):
                    e = i * RING + r
                    if not first:
                        end = pool.value_load(state["ends"][0:1, bass.ds(e - RING, 1)], min_val=0, max_val=SLOTS)
                        pool.wait_ge(s_y, end + 1)
                        pool.sem_inc(s_passed, 1)
                    pool.wait_ge(s_wd[r], i * 48 + 48)
                    pool.sem_inc(s_passed, 1)
                    pool.tensor_copy(ring[0][:, r, :], stage[:, r, :]).then_inc(s_whi, 1)
                    pool.wait_ge(s_whi, e + 1)
                    pool.tensor_tensor(ring[1][:, r, :], stage[:, r, :], ring[0][:, r, :].bitcast(F32), ALU.subtract)\
                        .then_inc(s_wlo, 1)

                for r in range(RING):
                    split(0, r, True)
                with pool.Fori(1, E1 // RING) as i:
                    for r in range(RING):
                        split(i, r, False)

            @block.scalar
            def _(act):
                def load_x(base, u):
                    act.dma_start(xs[:, u, :], rows_dram[bass.ds((base + u) * P, P), :]).then_inc(s_xs[u], 16)

                def x_high(base, u):
                    n = base + u
                    act.wait_ge(s_xt, n + 1)
                    act.activation(xT[0][:, u % 2, :], XB[u % 2][:, 0:D], ACT.Copy).then_inc(s_xhi, 1)

                def h_high(base, u):
                    n = base + u
                    act.wait_ge(s_ht, n + 1)
                    act.activation(hT[0][:, u % 2, 0:P], HB[u % 2][:, 0:P], ACT.Copy)
                    act.activation(hT[0][0:REST, u % 2, P:2 * P], HB[u % 2][0:REST, P:2 * P], ACT.Copy).then_inc(s_hhi, 1)

                def y_out(base, u):
                    n = base + u
                    act.wait_ge(s_y, n + 2)
                    if not (isinstance(base, int) and base < STEP):
                        act.wait_ge(s_ys[u], (base // STEP) * 16 if isinstance(base, int) else ys_count(base))
                    act.activation(ys[:, u, :], YB[u % 2][:, 0:D], ACT.Copy).then_inc(s_yc, 1)
                    act.wait_ge(s_yc, n + 1)
                    act.dma_start(y_dram[bass.ds(n * P, P), :], ys[:, u, :]).then_inc(s_ys[u], 16)

                def ys_count(base):
                    return base * (16 // STEP)

                def before(base, u, k):
                    return (base, u - k) if u >= k else (base - STEP, u - k + STEP)

                for u in range(STEP):
                    load_x(0, u)
                x_high(0, 0)

                def step(base, u, first, last):
                    if not (last and u == STEP - 1):
                        x_high(*((base, u + 1) if u < STEP - 1 else (base + STEP, 0)))
                    act.wait_ge(s_gu, base + u + 1)
                    act.activation(th[:, u % 2, :], GB[u % 2][:, 0:INNER], ACT.Tanh, scale=0.5).then_inc(s_th, 1)
                    if not last:
                        load_x(base + STEP, u)
                    if not (first and u < 1):
                        h_high(*before(base, u, 1))
                    if not (first and u < 2):
                        y_out(*before(base, u, 2))

                for u in range(STEP):
                    step(0, u, True, False)
                with act.Fori(1, SLOTS // STEP - 1) as i:
                    for u in range(STEP):
                        step(i * STEP, u, False, False)
                for u in range(STEP):
                    step(SLOTS - STEP, u, False, True)
                y_out(SLOTS - STEP, STEP - 2)
                h_high(SLOTS - STEP, STEP - 1)
                y_out(SLOTS - STEP, STEP - 1)
                for u in range(STEP):
                    act.wait_ge(s_ys[u], SLOTS // STEP * 16)

            @block.vector
            def _(dve):
                def x_low(base, u):
                    dve.wait_ge(s_xhi, base + u + 1)
                    dve.tensor_tensor(xT[1][:, u % 2, :], XB[u % 2][:, 0:D], xT[0][:, u % 2, :].bitcast(F32), ALU.subtract)\
                        .then_inc(s_xlo, 1)

                def hidden(base, u):
                    n, b = base + u, u % 2
                    dve.wait_ge(s_th, n + 1)
                    dve.scalar_tensor_tensor(gg[:, b, :], th[:, b, :], 1.0, GB[b][:, 0:INNER], ALU.add, ALU.mult).then_inc(s_gg, 1)
                    dve.wait_ge(s_gg, n + 1)
                    dve.scalar_tensor_tensor(hh[:, b, :], gg[:, b, :], 0.5, GB[b][:, INNER:2 * INNER], ALU.mult, ALU.mult)\
                        .then_inc(s_hh, 1)

                def h_low(base, u):
                    n, b = base + u, u % 2
                    dve.wait_ge(s_hhi, n + 1)
                    dve.tensor_tensor(hT[1][:, b, 0:P], HB[b][:, 0:P], hT[0][:, b, 0:P].bitcast(F32), ALU.subtract)
                    dve.tensor_tensor(hT[1][0:REST, b, P:2 * P], HB[b][0:REST, P:2 * P], hT[0][0:REST, b, P:2 * P].bitcast(F32),
                                      ALU.subtract).then_inc(s_hlo, 1)

                def step(base, u, first, last):
                    if not (last and u == STEP - 1):
                        x_low(*((base, u + 1) if u < STEP - 1 else (base + STEP, 0)))
                    hidden(base, u)
                    if not (first and u < 1):
                        h_low(*((base, u - 1) if u else (base - STEP, STEP - 1)))

                x_low(0, 0)
                for u in range(STEP):
                    step(0, u, True, False)
                with dve.Fori(1, SLOTS // STEP - 1) as i:
                    for u in range(STEP):
                        step(i * STEP, u, False, False)
                for u in range(STEP):
                    step(SLOTS - STEP, u, False, True)
                h_low(SLOTS - STEP, STEP - 1)

            @block.tensor
            def _(pe):
                def x_transposes(base, u, first):
                    n, b = base + u, u % 2
                    pe.wait_ge(s_xs[u], base * (16 // STEP) + 16)
                    if not (first and u < 2):
                        pe.wait_ge(s_xlo, n - 1)
                    for k in range(KD):
                        last = pe.transpose(XB[b][:, k * P:(k + 1) * P], xs[:, u, k * P:(k + 1) * P], ident)
                    last.then_inc(s_xt, 1)

                def place_of(n):
                    return pe.value_load(state["place"][0:1, bass.ds(n, 1)], min_val=0, max_val=RING - 1)

                def gate_up(base, u, first):
                    n, b = base + u, u % 2
                    owner = pe.value_load(state["owner"][0:1, bass.ds(n, 1)], min_val=0, max_val=E1 - 1)
                    place = place_of(n)
                    pe.wait_ge(s_wlo, owner + 2)
                    pe.wait_ge(s_xlo, n + 1)
                    if not (first and u < 2):
                        pe.wait_ge(s_hh, n - 1)
                    for k in range(KD):
                        c = k * 2 * INNER
                        last = product3(pe, GB[b][:, 0:2 * INNER], [a[:, b, k * P:(k + 1) * P] for a in xT],
                                        [w[:, bass.ds(place, 1), c:c + 2 * INNER] for w in ring], k == 0, k == KD - 1)
                    last.then_inc(s_gu, 1)

                def h_transposes(base, u, first):
                    n, b = base + u, u % 2
                    pe.wait_ge(s_hh, n + 1)
                    if not (first and u < 2):
                        pe.wait_ge(s_hlo, n - 1)
                    pe.transpose(HB[b][:, 0:P], hh[:, b, 0:P], ident)
                    pe.transpose(HB[b][0:REST, P:2 * P], hh[:, b, P:INNER], ident).then_inc(s_ht, 1)

                def down(base, u, first):
                    n, b = base + u, u % 2
                    place = place_of(n)
                    pe.wait_ge(s_hlo, n + 1)
                    if not (first and u < 2):
                        pe.wait_ge(s_yc, n - 1)
                    product3(pe, YB[b][:, 0:D], [a[:, b, 0:P] for a in hT],
                             [w[:, bass.ds(place, 1), GU:GU + D] for w in ring], True, False)
                    product3(pe, YB[b][:, 0:D], [a[0:REST, b, P:2 * P] for a in hT],
                             [w[0:REST, bass.ds(place, 1), GU + D:WE] for w in ring], False, True).then_inc(s_y, 1)

                def step(base, u, first, last):
                    def before(k):
                        return (base, u - k, first) if u >= k else (base - STEP, u - k + STEP, False)

                    if not (last and u == STEP - 1):
                        x_transposes(*((base, u + 1, first) if u < STEP - 1 else (base + STEP, 0, False)))
                    gate_up(base, u, first)
                    if not (first and u < 1):
                        h_transposes(*before(1))
                    if not (first and u < 2):
                        down(*before(2))

                x_transposes(0, 0, True)
                for u in range(STEP):
                    step(0, u, True, False)
                with pe.Fori(1, SLOTS // STEP - 1) as i:
                    for u in range(STEP):
                        step(i * STEP, u, False, False)
                for u in range(STEP):
                    step(SLOTS - STEP, u, False, True)
                down(SLOTS - STEP, STEP - 2, False)
                h_transposes(SLOTS - STEP, STEP - 1, False)
                down(SLOTS - STEP, STEP - 1, False)

        with ExitStack() as run:
            back = run.enter_context(nc.sbuf_tensor("e_back", [P, TILES, TOPK, D], F32))
            s_back = [sem(f"back{t}") for t in range(TILES)]
            s_sum, s_out = sem("sum"), sem("out")
            block = run.enter_context(nc.Block())

            @block.gpsimd
            def _(pool):
                for t in range(TILES):
                    for k in range(TOPK):
                        pool.indirect_dma_start(out=back[:, t, k, :], out_offset=None, in_=y_dram,
                                                in_offset=bass.IndirectOffsetOnAxis(pos[:, k, t:t + 1], 0)).then_inc(s_back[t], 16)

            @block.vector
            def _(dve):
                for k in range(TOPK):
                    pass
                for t in range(TILES):
                    dve.wait_ge(s_back[t], TOPK * 16)
                    for k in range(TOPK):
                        dve.scalar_tensor_tensor(acc[:, t, :], back[:, t, k, :], state["share"][:, t, k:k + 1], acc[:, t, :],
                                                 ALU.mult, ALU.add).then_inc(s_sum, 1)
                        dve.wait_ge(s_sum, TOPK * t + k + 1)

            @block.sync
            def _(sp):
                for t in range(TILES):
                    sp.wait_ge(s_sum, TOPK * (t + 1))
                    b, r = divmod(t, NT)
                    sp.dma_start(out[b, r * P:(r + 1) * P, :], acc[:, t, :]).then_inc(s_out, 16)
                sp.wait_ge(s_out, TILES * 16)


def build(nc, x, w0, wb, wd, vec, const, w1, ws, vec1, wg, wdn, out):
    with ExitStack() as ctx:
        state = {"con": ctx.enter_context(nc.sbuf_tensor("con", [P, NC], F32)),
                 "mhalf": ctx.enter_context(nc.sbuf_tensor("mhalf", [P, NT], F32)),
                 "s_zero": ctx.enter_context(nc.semaphore("s_zero")), "fills": ROWS // (P * FILL)}
        x1_dram = nc.dram_tensor("x1_dram", (B, T, D), F32, kind="Internal").ap()
        rows_dram = nc.dram_tensor("rows_dram", (ROWS, D), F32, kind="Internal").ap()
        y_dram = nc.dram_tensor("y_dram", (ROWS, D), F32, kind="Internal").ap()
        layer0(nc, state, x, w0, wb, wd, vec, const, x1_dram)
        for name, shape in (("xrows", [P, TILES, D]), ("acc", [P, TILES, D]), ("choice", [P, TILES, TOPK]),
                            ("chosen", [P, TILES, E1]), ("share", [P, TILES, TOPK])):
            state[name] = ctx.enter_context(nc.sbuf_tensor(name, shape, F32))
        state["pos"] = ctx.enter_context(nc.sbuf_tensor("pos", [P, TOPK, TILES], U32))
        for name, n in (("owner", SLOTS), ("place", SLOTS), ("ends", E1)):
            state[name] = ctx.enter_context(nc.sbuf_tensor(name, [1, n], I32))
        zeros = ctx.enter_context(nc.sbuf_tensor("zeros", [P, FILL * D], F32))
        state["zeros"], state["rows_dram"] = zeros, rows_dram
        layer1(nc, state, x1_dram, w1, ws, vec1)
        dispatch(nc, state)
        experts(nc, state, wg, wdn, rows_dram, y_dram, out)


def kernel(**a):
    import numpy as _np
    import concourse.bacc as _bacc
    from concourse import mybir as _mybir
    from concourse.bass_utils import run_bass_kernel_spmd as _run

    a = {k: _np.asarray(v) for k, v in a.items()}
    L0, F0 = "L0_attn_", "L0_ffn_"

    def experts_in(single, many):
        return [single, many.transpose(1, 0, 2).reshape(many.shape[1], -1)]

    def experts_out(single, many):
        return _np.concatenate([single, many.reshape(-1, many.shape[2])], axis=0)

    w0 = _np.concatenate([a[F0 + "W_gate"], a[F0 + "W_up"], a[L0 + "Wo"]]
                         + experts_in(a[F0 + "sA_gate"], a[F0 + "A_gate"]) + experts_in(a[F0 + "sA_up"], a[F0 + "A_up"])
                         + [a[L0 + "Wv"], a[F0 + "W_router"], a[L0 + "Wq"], a[L0 + "Wk"]], axis=1)
    wb = _np.concatenate([experts_out(a[F0 + "sB_" + n], a[F0 + "B_" + n]) for n in ("gate", "up", "down")], axis=1)
    wd = _np.concatenate([a[F0 + "W_down"]] + experts_in(a[F0 + "sA_down"], a[F0 + "A_down"]), axis=1)
    vec = _np.concatenate([a[L0 + "bo"], a[F0 + "expert_bias"]])
    A1, F1 = "L1_attn_", "L1_ffn_"
    g, u = a[F1 + "shared_gate_w"].T, a[F1 + "shared_up_w"].T
    w1 = _np.concatenate([a[A1 + "qkv"], a[A1 + "o_proj"], g, u[:, P:], u[:, :P], a[F1 + "router_w"].T,
                          a[A1 + "gamma"][:, None], a[A1 + "beta"][:, None]], axis=1)
    ws = a[F1 + "shared_down_w"].T
    vec1 = a[F1 + "router_b"]
    ins = {"x": a[L0 + "x"], "w0": w0, "wb": wb, "wd": wd, "vec": vec, "const": constants(),
           "w1": w1, "ws": ws, "vec1": vec1,
           "wg": _np.concatenate([m.transpose(0, 2, 1) for m in (a[F1 + "gate_w"], a[F1 + "up_w"])],
                                 axis=2),
           "wdn": a[F1 + "down_w"].transpose(0, 2, 1)}

    nc = _bacc.Bacc("TRN2", target_bir_lowering=False, num_devices=1)
    arrays = {f"in_{n}": _np.ascontiguousarray(v) for n, v in ins.items()}
    args = [nc.dram_tensor(n, v.shape, _mybir.dt.from_np(v.dtype), kind="ExternalInput").ap() for n, v in arrays.items()]
    args.append(nc.dram_tensor("out_0", (B, T, D), _mybir.dt.float32, kind="ExternalOutput").ap())
    build(nc, *args)
    r = _run(nc, [arrays], core_ids=[0])
    return r.results[0]["out_0"]
```
